# Optimizing a Trainium2 kernel written in Bass

```python
import numpy as np
import jax
import jax.numpy as jnp

def _softmax(x, axis=-1):
    return jax.nn.softmax(x, axis=axis)

def _gelu(x):
    return jax.nn.gelu(x, approximate=True)

def _silu(x):
    return jax.nn.silu(x)

def _sigmoid(x):
    return jax.nn.sigmoid(x)

def _layernorm(x, axis=-1, eps=1e-05):
    m = jnp.mean(x, axis=axis, keepdims=True)
    v = jnp.var(x, axis=axis, keepdims=True)
    return (x - m) / jnp.sqrt(v + eps)

def _scatter_add(tgt, idx, src, axis=0):
    return tgt.at[idx].add(src)

def _segment_sum(src, seg, n):
    return jax.ops.segment_sum(src, seg, n)
kernel_name = 'mk_decoder_postln_d1_seqx_r8_a3f4e9'

def setup_inputs(seed: int=0):
    np.random.seed(seed)
    _w = jnp.asarray

    def _rec_inputs():
        import jax
        import jax.numpy as jnp
        _rk = jax.random.key(seed)
        x = 7.22e-05 + 1 * jax.random.normal(jax.random.fold_in(_rk, 1), (4, 256, 256), jnp.float32)
        _lenS = 256 - jax.random.randint(jax.random.fold_in(_rk, 7), (4,), 0, max(1, 256 // 4) + 1, jnp.int32)
        _lenS2 = 256 - jax.random.randint(jax.random.fold_in(_rk, 8), (4,), 0, max(1, 256 // 4) + 1, jnp.int32)
        _ctx_2048P = jax.random.normal(jax.random.fold_in(_rk, 11), (4, 16, 256), jnp.float32)
        _ctx_2048c = jax.random.dirichlet(jax.random.fold_in(_rk, 511), 0.3 * jnp.ones((16,), jnp.float32), (4, 256))
        _ctx_2048t = jnp.einsum('bsk,bkd->bsd', _ctx_2048c, _ctx_2048P)
        _ctx_2048t = _ctx_2048t * jax.lax.rsqrt(jnp.mean(jnp.square(_ctx_2048t)) + 1e-12) * 0.953939
        ctx_2048 = 4.13588e-05 + 0.999923 * (_ctx_2048t + 0.3 * jax.random.normal(jax.random.fold_in(_rk, 611), (4, 256, 256), jnp.float32))
        return (x, ctx_2048)
    x, ctx_2048 = _rec_inputs()

    def _L0_attn_setup():
        import jax, jax.numpy as jnp
        import numpy as np
        B, N, E, HD = (4, 256, 256, 128)
        E2 = 2 * E
        EPS = 1e-06
        key = jax.random.key(seed)
        ks = jax.random.split(key, 7)
        s = 0.02
        return {'x': jax.random.normal(ks[0], (B, N, E), dtype=jnp.float32), 'Wq1': jax.random.normal(ks[1], (E, HD), dtype=jnp.float32) * s, 'Wq2': jax.random.normal(ks[2], (HD, E2), dtype=jnp.float32) * s, 'Wk1': jax.random.normal(ks[3], (E, HD), dtype=jnp.float32) * s, 'Wk2': jax.random.normal(ks[4], (HD, E2), dtype=jnp.float32) * s, 'Wv': jax.random.normal(ks[5], (E, E2), dtype=jnp.float32) * s, 'Wo': jax.random.normal(ks[6], (E2, E), dtype=jnp.float32) * s, 'norm_w': jnp.ones((E2,), dtype=jnp.float32)}
    _L0_attn_all = _L0_attn_setup()
    _L0_attn_in = {k: v for k, v in _L0_attn_all.items() if k in ('Wq1', 'Wq2', 'Wk1', 'Wk2', 'Wv', 'Wo', 'norm_w')}
    del _L0_attn_all

    def _L0_xattn_setup():
        import jax, jax.numpy as jnp
        import numpy as np
        N_HEAD = 8
        key = jax.random.key(seed)
        k1, k2, k3 = jax.random.split(key, 3)
        b, d, m = (4, 128, 256)
        c, n = (128, 256)
        q = jax.random.normal(k1, (b, d, m), dtype=jnp.float32)
        k = jax.random.normal(k2, (d // d * b, d, n), dtype=jnp.float32).reshape(b, d, n)
        v = jax.random.normal(k3, (b, c, n), dtype=jnp.float32)
        return {'q': q, 'k': k, 'v': v}
    _L0_xattn_all = _L0_xattn_setup()
    _L0_xattn_in = {k: v for k, v in _L0_xattn_all.items() if k in ()}
    del _L0_xattn_all

    def _L0_ffn_setup():
        import jax, jax.numpy as jnp
        import numpy as np
        DIM_IN = 256
        DIM_HIDDEN = 1024
        key = jax.random.key(seed)
        k_x, k_g, k_u, k_d = jax.random.split(key, 4)
        s_in = 1.0 / np.sqrt(DIM_IN)
        s_hid = 1.0 / np.sqrt(DIM_HIDDEN)
        x = jax.random.normal(k_x, (4, 256, DIM_IN), dtype=jnp.float32)
        w_gate = jax.random.uniform(k_g, (DIM_HIDDEN, DIM_IN), jnp.float32, -s_in, s_in)
        w_up = jax.random.uniform(k_u, (DIM_HIDDEN, DIM_IN), jnp.float32, -s_in, s_in)
        w_down = jax.random.uniform(k_d, (DIM_IN, DIM_HIDDEN), jnp.float32, -s_hid, s_hid)
        return {'x': x, 'w_gate': w_gate, 'w_up': w_up, 'w_down': w_down}
    _L0_ffn_all = _L0_ffn_setup()
    _L0_ffn_in = {k: v for k, v in _L0_ffn_all.items() if k in ('w_gate', 'w_up', 'w_down')}
    del _L0_ffn_all
    return {'x': x, 'ctx_2048': ctx_2048, 'L0_attn_Wq1': _L0_attn_in['Wq1'], 'L0_attn_Wq2': _L0_attn_in['Wq2'], 'L0_attn_Wk1': _L0_attn_in['Wk1'], 'L0_attn_Wk2': _L0_attn_in['Wk2'], 'L0_attn_Wv': _L0_attn_in['Wv'], 'L0_attn_Wo': _L0_attn_in['Wo'], 'L0_attn_norm_w': _L0_attn_in['norm_w'], 'L0_ffn_w_gate': _L0_ffn_in['w_gate'], 'L0_ffn_w_up': _L0_ffn_in['w_up'], 'L0_ffn_w_down': _L0_ffn_in['w_down']}

def reference(x, ctx_2048, L0_attn_Wq1, L0_attn_Wq2, L0_attn_Wk1, L0_attn_Wk2, L0_attn_Wv, L0_attn_Wo, L0_attn_norm_w, L0_ffn_w_gate, L0_ffn_w_up, L0_ffn_w_down):
    import jax
    import jax.numpy as jnp

    def _L0_attn_ref(x, Wq1, Wq2, Wk1, Wk2, Wv, Wo, norm_w):
        import jax, jax.numpy as jnp
        import numpy as np
        B, N, E, HD = (4, 256, 256, 128)
        E2 = 2 * E
        EPS = 1e-06
        q = jax.nn.silu(x @ Wq1 @ Wq2)
        log_f_raw = x @ Wk1 @ Wk2
        v = x @ Wv
        f = jax.nn.sigmoid(log_f_raw)
        log_f = jax.nn.log_sigmoid(f)
        a = jnp.exp(log_f)
        k = 1.0 - a

        def combine(c1, c2):
            a1, b1 = c1
            a2, b2 = c2
            return (a1 * a2, a2 * b1 + b2)
        _, h = jax.lax.associative_scan(combine, (a, k * v), axis=1)
        out = q * h
        out = out * jax.lax.rsqrt(jnp.mean(out * out, axis=-1, keepdims=True) + EPS)
        out = out * norm_w
        return out @ Wo

    def _L0_xattn_ref(q, k, v):
        import jax, jax.numpy as jnp
        import numpy as np
        N_HEAD = 8
        b, d, m = q.shape
        c = v.shape[1]
        h = N_HEAD
        qh = q.reshape(b * h, d // h, m)
        kh = k.reshape(b * h, d // h, -1)
        vh = v.reshape(b * h, c // h, -1)
        scale = 1.0 / jnp.sqrt(jnp.asarray(d // h, dtype=q.dtype))
        qk = jnp.einsum('bdm,bdn->bmn', qh, kh) * scale
        sm = jax.nn.softmax(qk, axis=-1)
        ret = jnp.einsum('bmn,bcn->bcm', sm, vh)
        return ret.reshape(b, c, m)

    def _L0_ffn_ref(x, w_gate, w_up, w_down):
        import jax, jax.numpy as jnp
        import numpy as np
        DIM_IN = 256
        DIM_HIDDEN = 1024
        gate = jnp.einsum('bsd,hd->bsh', x, w_gate)
        up = jnp.einsum('bsd,hd->bsh', x, w_up)
        gated = jax.nn.silu(gate) * up
        return jnp.einsum('bsh,dh->bsd', gated, w_down)
    x = _layernorm(x + _L0_attn_ref(x, L0_attn_Wq1, L0_attn_Wq2, L0_attn_Wk1, L0_attn_Wk2, L0_attn_Wv, L0_attn_Wo, L0_attn_norm_w), axis=-1)
    x = _layernorm(x + _L0_xattn_ref(x, ctx_2048, ctx_2048), axis=-1)
    x = _layernorm(x + _L0_ffn_ref(x, L0_ffn_w_gate, L0_ffn_w_up, L0_ffn_w_down), axis=-1)
    return x

_drawn_inputs = setup_inputs


def setup_inputs(seed=0):
    import zlib

    import numpy as np

    out = dict(_drawn_inputs(seed))
    spreads = {'L0_attn_norm_w': (1.0, 0.2)}
    factors = {'L0_attn_Wk1': 8.0, 'L0_attn_Wk2': 8.0}
    for name, (base, spread) in spreads.items():
        noise = np.random.default_rng([zlib.crc32(name.encode()), seed]).standard_normal(out[name].shape)
        drawn = base * np.exp(spread * noise) if base else spread * noise
        out[name] = jnp.asarray(drawn.astype(out[name].dtype))
    for name, factor in factors.items():
        out[name] = (out[name] * factor).astype(out[name].dtype)
    return out
```

```python
from contextlib import ExitStack

import concourse.bass as bass
from concourse import mybir

F32 = mybir.dt.float32
F32R = mybir.dt.float32r
ALU = mybir.AluOpType
ACT = mybir.ActivationFunctionType
AX_X = mybir.AxisListType.X

P = 128
B = 4
T = 256
TT = T // P
E = 256
EC = E // P
HD = 128
C = 512
CC = C // P
H = 8
D = T // H
Q = P // D
HP = H // 2
F = 1024
FC = F // P
FP = FC // 2
RMS_EPS = 1e-6
LN_EPS = 1e-5
STACK = 3 * D
ROWS = STACK + 2
ATT_SCALE = float(D) ** -0.5

PLAN = {
    "mix": [0.0, 11.0, 22.0, 34.0],
    "att": [18.0, 31.0, 44.0, 60.0],
    "ffn": [46.0, 62.0, 80.0, 100.0],
}


def in_order(steps):
    out = []
    for phase, at, name, parts, each in steps:
        for b in range(B):
            for i in range(parts):
                out.append((PLAN[phase][b] + at + i * each, len(out), name, b, i))
    return [(name, b, i) for _, _, name, b, i in sorted(out)]


PE_STEPS = [
    ("mix", 0.0, "low", 1, 0), ("mix", 3.2, "value", 1, 0), ("mix", 1.6, "decay", 1, 0),
    ("mix", 5.9, "query", 1, 0), ("mix", 14.0, "squares", 1, 0), ("mix", 15.0, "mixed", 1, 0),
    ("att", 5.0, "scores", HP, 1.0), ("att", 10.0, "turn_max", 1, 0), ("att", 14.0, "shifted", HP, 1.0),
    ("att", 19.0, "sums", 1, 0), ("att", 20.0, "context", 1, 0), ("att", 25.0, "turn_x", 1, 0),
    ("ffn", 0.0, "hidden", FP, 3.0), ("ffn", 13.0, "down", 1, 0),
]
PAIR_KINDS = ("value", "decay", "query", "scores", "shifted", "hidden")


def decoder_layer(nc, xT, x, ctx, ctxT, wq1, wq2, wk1, wk2, wv, wo, norm, gateT, upT, downT, out):
    with ExitStack() as stack:
        def sb(name, shape, dt=F32):
            return stack.enter_context(nc.sbuf_tensor(name, shape, dt))

        def sem(name):
            return stack.enter_context(nc.semaphore(name))

        def halves(name, shape):
            return sb(name + "_hi", shape, F32R), sb(name + "_lo", shape, F32R)

        w_low = halves("w_low", [P, 2, EC, HD])
        w_high = halves("w_high", [P, 2, C])
        w_v = halves("w_v", [P, EC, C])
        w_o = halves("w_o", [P, CC, E])
        w_gate = halves("w_gate", [P, EC, F])
        w_up = halves("w_up", [P, EC, F])
        w_down = halves("w_down", [P, FC, E])
        prob = sb("prob", [P, H, EC, E])
        raw = prob[:, :, :, :].rearrange("p (s h) c e -> p s (h c e)", s=4)
        normw = sb("normw", [P, CC])

        res = sb("res", [P, B, TT, E])
        xt_raw = sb("xt_raw", [P, 2, EC, T])
        xt = halves("xt", [P, 2, EC, T])
        low = halves("low", [P, 2, T])
        tan = sb("tan", [P, CC, T])
        dec = sb("dec", [P, CC, T])
        hid = sb("hid", [P, CC, T])
        gat = sb("gat", [P, CC, T])
        o = halves("o", [P, CC, T])
        ctx_raw = sb("ctx_raw", [P, TT, E])
        ctx_h = halves("ctx_h", [P, TT, E])
        x1_h = halves("x1_h", [P, TT, E])
        ctx_t = sb("ctx_t", [P, B, EC, T])
        c_stack = sb("c_stack", [P, H, E], F32R)
        x_stack = sb("x_stack", [P, H, E], F32R)
        top = sb("top", [P, H, EC])
        neg = halves("neg", [2 * H, P])
        sum_t = sb("sum_t", [P, E // 32, 32])
        inv = sb("inv", [P, TT, E // 32])
        inv_b = sb("inv_b", [P, TT, E])
        x2t = halves("x2t", [P, EC, T])
        gu = sb("gu", [P, 2, 2 * T])
        g = halves("g", [P, FC, T])
        ident = sb("ident", [P, P])
        ones = sb("ones", [P, D])
        pick = sb("pick", [P, TT, D])
        quarter = sb("quarter", [P, 1])
        power = sb("power", [P, TT])
        sq_t = sb("sq_t", [P, TT, 32])
        ms = sb("ms", [P, TT])
        rms = sb("rms", [P, TT])
        bn = sb("bn", [P, 3, TT, 6])
        mv = sb("mv", [P, 3, TT, 2])
        ve = sb("ve", [P, 3, TT])
        rstd = sb("rstd", [P, 3, TT])

        pair = [stack.enter_context(nc.psum_tensor(f"pair{i}", [P, 4, 256], F32)) for i in range(3)]
        single = [stack.enter_context(nc.psum_tensor(f"single{i}", [P, 512], F32)) for i in range(2)]

        in_xt, in_x, in_ctx, in_ctxt = sem("in_xt0"), sem("in_x"), sem("in_ctx"), sem("in_ctxt")
        in_xt = [in_xt, sem("in_xt1")]
        in_low, in_high, in_v, in_o, in_norm = (sem(n) for n in ("in_low", "in_high", "in_v", "in_o", "in_norm"))
        in_ffn = [sem(f"in_ffn{c}") for c in range(6)]
        low_w_hi, low_w_lo = sem("low_w_hi"), sem("low_w_lo")
        high_w_hi, high_w_lo = sem("high_w_hi"), sem("high_w_lo")
        v_w_hi, v_w_lo = sem("v_w_hi"), sem("v_w_lo")
        o_scaled, o_w_hi, o_w_lo = sem("o_scaled"), sem("o_w_hi"), sem("o_w_lo")
        ffn_w_hi, ffn_w_lo = sem("ffn_w_hi"), sem("ffn_w_lo")
        xt_hi, xt_lo = sem("xt_hi"), sem("xt_lo")
        consts, const_v = sem("consts"), sem("const_v")
        low_done, low_hi, low_lo = sem("low_done"), sem("low_hi"), sem("low_lo")
        value_done, decay_done, query_done = sem("value_done"), sem("decay_done"), sem("query_done")
        tan1, tan2, dec_done, kv_done = sem("tan1"), sem("tan2"), sem("dec_done"), sem("kv_done")
        state_done, qtan, silu_done, out_done = sem("state_done"), sem("qtan"), sem("silu_done"), sem("out_done")
        sq_done, o_hi, o_lo = sem("sq_done"), sem("o_hi"), sem("o_lo")
        squares_done, sq_turned, ms_done, rms_done = sem("squares_done"), sem("sq_turned"), sem("ms_done"), sem("rms_done")
        mixed_done = sem("mixed_done")
        added = [sem(f"added{n}") for n in range(3)]
        bn_done = [sem(f"bn_done{n}") for n in range(3)]
        mv_done = [sem(f"mv_done{n}") for n in range(3)]
        ve_done = [sem(f"ve_done{n}") for n in range(3)]
        rstd_done = [sem(f"rstd_done{n}") for n in range(3)]
        normed = [sem(f"normed{n}") for n in range(3)]
        ctx_hi, ctx_lo, ctx_stacked = sem("ctx_hi"), sem("ctx_lo"), sem("ctx_stacked")
        x1_hi, x1_lo, x_stacked = sem("x1_hi"), sem("x1_lo"), sem("x_stacked")
        scores_done, top_done, top_turned = sem("scores_done"), sem("top_done"), sem("top_turned")
        neg_hi, neg_lo, neg_stacked = sem("neg_hi"), sem("neg_lo"), sem("neg_stacked")
        shifted_done, exp_done, sums_done, context_done = sem("shifted_done"), sem("exp_done"), sem("sums_done"), sem("context_done")
        sum_turned, inv_done, inv_spread, weighed = sem("sum_turned"), sem("inv_done"), sem("inv_spread"), sem("weighed")
        x_turned, x2_hi, x2_lo = sem("x_turned"), sem("x2_hi"), sem("x2_lo")
        hidden_done, gtan, gate_done, g_done = sem("hidden_done"), sem("gtan"), sem("gate_done"), sem("g_done")
        g_hi, g_lo, down_done = sem("g_hi"), sem("g_lo"), sem("down_done")
        stored = sem("stored")

        freed_by = {"value": kv_done, "decay": tan1, "query": silu_done, "scores": top_done,
                    "shifted": exp_done, "hidden": g_done, "low": low_lo, "squares": sq_turned,
                    "mixed": added[0], "turn_max": neg_lo, "sums": sum_turned, "context": weighed,
                    "turn_x": x2_lo, "down": added[2]}
        parts_of = {s[2]: s[3] for s in PE_STEPS}
        place, before = {}, {}
        for ring, kinds in ((pair, True), (single, False)):
            held = [None] * len(ring)
            n = 0
            for step in in_order(PE_STEPS):
                if (step[0] in PAIR_KINDS) == kinds:
                    place[step] = ring[n % len(ring)]
                    before[step] = held[n % len(ring)]
                    held[n % len(ring)] = step
                    n += 1

        def wait_freed(pe, step):
            if before[step] is not None:
                kind, b, i = before[step]
                pe.wait_ge(freed_by[kind], parts_of[kind] * b + i + 1)

        stacks = 16 * 3 * Q

        block = stack.enter_context(nc.Block())

        @block.sync
        def _(sp):
            xT_v = xT.rearrange("(c p) (b t) -> b p c t", p=P, b=B)
            x_v = x.rearrange("b (t p) e -> b p t e", p=P)
            ctx_v = ctx.rearrange("b (t p) e -> b p t e", p=P)
            ctxT_v = ctxT.rearrange("(c p) (b t) -> b p c t", p=P, b=B)
            out_v = out.rearrange("b (t p) e -> b p t e", p=P)
            raw_low = raw[:, 0, 0:2 * EC * HD].rearrange("p (w c n) -> p w c n", w=2, c=EC)

            def load_xt(b):
                if b >= 2:
                    sp.wait_ge(xt_lo, b - 1)
                sp.dma_start(xt_raw[:, b % 2, :, :], xT_v[b]).then_inc(in_xt[b % 2], 16)

            def load_x(b):
                sp.dma_start(res[:, b, :, :], x_v[b]).then_inc(in_x, 16)

            def load_ctx(b):
                if b >= 1:
                    sp.wait_ge(ctx_lo, b)
                sp.dma_start(ctx_raw[:, :, :], ctx_v[b]).then_inc(in_ctx, 16)

            def stack_rows(dst, parts, b, done):
                for n, src in enumerate(parts):
                    for j in range(Q):
                        to = dst[n * D:(n + 1) * D, :, :].rearrange("p (t j) e -> p j t e", j=Q)[:, j]
                        sp.dma_start(to.bitcast(F32), src[j * D:(j + 1) * D, :, :].bitcast(F32)).then_inc(done, 16)

            def stack_ctx(b):
                sp.wait_ge(ctx_hi, b + 1)
                sp.wait_ge(ctx_lo, b + 1)
                if b >= 1:
                    sp.wait_ge(shifted_done, HP * b)
                stack_rows(c_stack, (ctx_h[0], ctx_h[1], ctx_h[0]), b, ctx_stacked)

            def stack_x(b):
                sp.wait_ge(x1_hi, b + 1)
                sp.wait_ge(x1_lo, b + 1)
                if b >= 1:
                    sp.wait_ge(shifted_done, HP * b)
                stack_rows(x_stack, (x1_h[0], x1_h[0], x1_h[1]), b, x_stacked)

            def stack_max(b):
                for n, ready in ((0, neg_hi), (1, neg_lo)):
                    sp.wait_ge(ready, b + 1)
                    if b >= 1 and n == 0:
                        sp.wait_ge(shifted_done, HP * b)
                    row = x_stack[STACK + n:STACK + n + 1, :, :].rearrange("p h (c m) -> p (h c) m", c=EC)
                    sp.dma_start(row.bitcast(F32), neg[n][:, :].bitcast(F32)).then_inc(neg_stacked, 16)

            def load_ffn(c):
                src = [gateT[0:P], gateT[P:2 * P], upT[0:P], upT[P:2 * P], downT[0:F // 2], downT[F // 2:F]][c]
                slot = c % 4
                if c < 4:
                    sp.wait_ge([low_w_lo, high_w_lo, v_w_lo, o_w_lo][c], 1)
                else:
                    sp.wait_ge(ffn_w_lo, c - 3)
                dst = raw[:, slot, :]
                if c >= 4:
                    dst, src = dst.rearrange("p (k n) -> p k n", n=E), src.rearrange("(k p) n -> p k n", p=P)
                sp.dma_start(dst, src).then_inc(in_ffn[c], 16)

            def store(b):
                sp.wait_ge(normed[2], b + 1)
                sp.dma_start(out_v[b], res[:, b, :, :]).then_inc(stored, 16)

            sp.dma_start(raw_low[:, 0, :, :], wq1.rearrange("(c p) n -> p c n", p=P)).then_inc(in_low, 16)
            sp.dma_start(raw_low[:, 1, :, :], wk1.rearrange("(c p) n -> p c n", p=P)).then_inc(in_low, 16)
            load_xt(0)
            sp.dma_start(raw[:, 2, :].rearrange("p (c n) -> p c n", c=EC), wv.rearrange("(c p) n -> p c n", p=P)).then_inc(in_v, 16)
            sp.dma_start(raw[:, 1, C:2 * C], wk2).then_inc(in_high, 16)
            sp.dma_start(raw[:, 1, 0:C], wq2).then_inc(in_high, 16)
            load_xt(1)
            sp.dma_start(normw[:, :], norm).then_inc(in_norm, 16)
            sp.dma_start(raw[:, 3, :].rearrange("p (c n) -> p c n", c=CC), wo.rearrange("(c p) n -> p c n", p=P)).then_inc(in_o, 16)
            load_x(0)
            load_ctx(0)
            stack_ctx(0)
            load_ffn(0)
            load_xt(2)
            load_ffn(1)
            load_ffn(2)
            load_x(1)
            load_ffn(3)
            for b in range(B):
                sp.dma_start(ctx_t[:, b, :, :], ctxT_v[b]).then_inc(in_ctxt, 16)
            load_ffn(4)
            load_ffn(5)
            load_x(2)
            load_x(3)
            stack_x(0)
            load_ctx(1)
            load_xt(3)
            stack_max(0)
            for b in range(1, B):
                stack_ctx(b)
                stack_x(b)
                if b + 1 < B:
                    load_ctx(b + 1)
                stack_max(b)
            for b in range(B):
                store(b)
            sp.wait_ge(stored, 16 * B)

        @block.tensor
        def _(pe):
            def product(dst, weights, moving, terms, last=None):
                n = 0
                for term in terms:
                    for wn, xn in ((0, 0), (0, 1), (1, 0)):
                        ins = nc.tensor.matmul(dst, weights[wn](term), moving[xn](term),
                                               start=(n == 0), stop=(n == 3 * len(terms) - 1))
                        n += 1
                return ins

            def low_proj(b, i):
                ps = place["low", b, i]
                pe.wait_ge(low_w_hi, 1)
                pe.wait_ge(low_w_lo, 1)
                pe.wait_ge(xt_hi, b + 1)
                pe.wait_ge(xt_lo, b + 1)
                for w in range(2):
                    ins = product(ps[:, w * T:(w + 1) * T], [lambda c, h=h: w_low[h][:, w, c, :] for h in (0, 1)],
                                  [lambda c, h=h: xt[h][:, b % 2, c, :] for h in (0, 1)], range(EC))
                ins.then_inc(low_done, 1)

            def value_proj(b, i):
                ps = place["value", b, i]
                pe.wait_ge(v_w_hi, 1)
                pe.wait_ge(v_w_lo, 1)
                for cc in range(CC):
                    ins = product(ps[:, cc, :], [lambda c, h=h: w_v[h][:, c, cc * P:(cc + 1) * P] for h in (0, 1)],
                                  [lambda c, h=h: xt[h][:, b % 2, c, :] for h in (0, 1)], range(EC))
                ins.then_inc(value_done, 1)

            def high_proj(kind, b, i):
                ps = place[kind, b, i]
                w, done = (0, query_done) if kind == "query" else (1, decay_done)
                pe.wait_ge(high_w_hi, 1)
                pe.wait_ge(high_w_lo, 1)
                pe.wait_ge(low_hi, b + 1)
                pe.wait_ge(low_lo, b + 1)
                for cc in range(CC):
                    ins = product(ps[:, cc, :], [lambda c, h=h: w_high[h][:, w, cc * P:(cc + 1) * P] for h in (0, 1)],
                                  [lambda c, h=h: low[h][:, w, :] for h in (0, 1)], range(1))
                ins.then_inc(done, 1)

            def squares(b, i):
                ps = place["squares", b, i]
                pe.wait_ge(const_v, 1)
                pe.wait_ge(sq_done, b + 1)
                sq = tan[:, :, :].rearrange("p c (t j d) -> p c t j d", t=TT, j=Q)
                for cc in range(CC):
                    for j in range(Q):
                        ins = nc.tensor.matmul(ps[j * D:(j + 1) * D, 0:TT * D], ones[:, :], sq[:, cc, :, j, :],
                                               start=(cc == 0), stop=(cc == CC - 1))
                ins.then_inc(squares_done, 1)

            def mixed(b, i):
                ps = place["mixed", b, i]
                pe.wait_ge(o_w_hi, 1)
                pe.wait_ge(o_w_lo, 1)
                pe.wait_ge(o_hi, b + 1)
                pe.wait_ge(o_lo, b + 1)
                for t in range(TT):
                    ins = product(ps[:, t * E:(t + 1) * E], [lambda c, h=h: o[h][:, c, t * P:(t + 1) * P] for h in (0, 1)],
                                  [lambda c, h=h: w_o[h][:, c, :] for h in (0, 1)], range(CC))
                ins.then_inc(mixed_done, 1)

            def scores(b, i):
                ps = place["scores", b, i]
                pe.wait_ge(ctx_stacked, stacks * (b + 1))
                pe.wait_ge(x_stacked, stacks * (b + 1))
                for h in range(2):
                    for c in range(EC):
                        ins = nc.tensor.matmul(ps[:, 2 * h + c, :], x_stack[0:STACK, 2 * i + h, c * P:(c + 1) * P],
                                               c_stack[0:STACK, 2 * i + h, :], start=True, stop=True)
                ins.then_inc(scores_done, 1)

            def turn_max(b, i):
                ps = place["turn_max", b, i]
                pe.wait_ge(consts, 7)
                pe.wait_ge(top_done, HP * (b + 1))
                nc.tensor.transpose(ps[0:2 * H, 0:P], top[:, :, :].rearrange("p h c -> p (h c)"), ident[:, :]).then_inc(top_turned, 1)

            def shifted(b, i):
                ps = place["shifted", b, i]
                pe.wait_ge(neg_stacked, 32 * (b + 1))
                for h in range(2):
                    for c in range(EC):
                        ins = nc.tensor.matmul(ps[:, 2 * h + c, :], c_stack[0:ROWS, 2 * i + h, c * P:(c + 1) * P],
                                               x_stack[0:ROWS, 2 * i + h, :], start=True, stop=True)
                ins.then_inc(shifted_done, 1)

            def sums(b, i):
                ps = place["sums", b, i]
                pe.wait_ge(exp_done, HP * (b + 1))
                for n in range(TT * EC):
                    t, c = n // EC, n % EC
                    for j in range(Q):
                        ins = nc.tensor.matmul(ps[j * D:(j + 1) * D, 0:E], pick[:, t, :], prob[:, Q * t + j, c, :],
                                               start=(n == 0), stop=(n == TT * EC - 1))
                ins.then_inc(sums_done, 1)

            def context(b, i):
                ps = place["context", b, i]
                if b == 0:
                    pe.wait_ge(in_ctxt, 16 * B)
                for t in range(TT):
                    for c in range(EC):
                        for j in range(Q):
                            first = t * P + j * D
                            ins = nc.tensor.matmul(ps[j * D:(j + 1) * D, t * E:(t + 1) * E],
                                                   ctx_t[:, b, c, first:first + D], prob[:, Q * t + j, c, :],
                                                   start=(c == 0), stop=(c == EC - 1))
                ins.then_inc(context_done, 1)

            def turn_x(b, i):
                ps = place["turn_x", b, i]
                pe.wait_ge(normed[1], b + 1)
                for c in range(EC):
                    for t in range(TT):
                        ins = nc.tensor.transpose(ps[:, c * T + t * P:c * T + (t + 1) * P],
                                                  res[:, b, t, c * P:(c + 1) * P], ident[:, :])
                ins.then_inc(x_turned, 1)

            def hidden(b, i):
                ps = place["hidden", b, i]
                if b == 0 and i == 0:
                    pe.wait_ge(ffn_w_lo, 4)
                pe.wait_ge(x2_hi, b + 1)
                pe.wait_ge(x2_lo, b + 1)
                for n, w in enumerate((w_gate, w_up)):
                    for k in range(2):
                        first = (2 * i + k) * P
                        ins = product(ps[:, 2 * n + k, :], [lambda c, h=h: w[h][:, c, first:first + P] for h in (0, 1)],
                                      [lambda c, h=h: x2t[h][:, c, :] for h in (0, 1)], range(EC))
                ins.then_inc(hidden_done, 1)

            def down(b, i):
                ps = place["down", b, i]
                if b == 0:
                    pe.wait_ge(ffn_w_lo, 6)
                pe.wait_ge(g_hi, FP * (b + 1))
                pe.wait_ge(g_lo, FP * (b + 1))
                for t in range(TT):
                    ins = product(ps[:, t * E:(t + 1) * E], [lambda c, h=h: g[h][:, c, t * P:(t + 1) * P] for h in (0, 1)],
                                  [lambda c, h=h: w_down[h][:, c, :] for h in (0, 1)], range(FC))
                ins.then_inc(down_done, 1)

            do = {"low": low_proj, "value": value_proj, "squares": squares, "mixed": mixed, "scores": scores,
                  "turn_max": turn_max, "shifted": shifted, "sums": sums, "context": context,
                  "turn_x": turn_x, "hidden": hidden, "down": down,
                  "decay": lambda b, i: high_proj("decay", b, i), "query": lambda b, i: high_proj("query", b, i)}
            for kind, b, i in in_order(PE_STEPS):
                wait_freed(pe, (kind, b, i))
                do[kind](b, i)

        @block.scalar
        def _(act):
            act.wait_ge(in_v, 16)
            nc.scalar.activation(w_v[0][:, :, :], raw[:, 2, :].rearrange("p (c n) -> p c n", c=EC), ACT.Copy).then_inc(v_w_hi, 1)
            act.wait_ge(in_high, 32)
            nc.scalar.activation(w_high[0][:, :, :], raw[:, 1, :].rearrange("p (w n) -> p w n", w=2), ACT.Copy).then_inc(high_w_hi, 1)

            def low_high(b, i):
                ps = place["low", b, 0]
                act.wait_ge(low_done, b + 1)
                if b >= 1:
                    act.wait_ge(query_done, b)
                nc.scalar.activation(low[0][:, :, :], ps[:, :].rearrange("p (w t) -> p w t", w=2), ACT.Copy).then_inc(low_hi, 1)

            def decay(b, i):
                ps = place["decay", b, 0]
                act.wait_ge(decay_done, b + 1)
                if b >= 1:
                    act.wait_ge(squares_done, b)
                if b == 0:
                    act.wait_ge(const_v, 1)
                nc.scalar.activation(tan[:, :, :], ps[:, :, :], ACT.Tanh, scale=0.5).then_inc(tan1, 1)
                act.wait_ge(tan1, b + 1)
                nc.scalar.activation(tan[:, :, :], tan[:, :, :], ACT.Tanh, bias=quarter[:, 0:1], scale=0.25).then_inc(tan2, 1)

            def query(b, i):
                ps = place["query", b, 0]
                act.wait_ge(query_done, b + 1)
                if b >= 1:
                    act.wait_ge(o_lo, b)
                    act.wait_ge(sq_done, b)
                nc.scalar.activation(gat[:, :, :], ps[:, :, :], ACT.Tanh, scale=0.5).then_inc(qtan, 1)

            def outputs(b, i):
                act.wait_ge(out_done, b + 1)
                act.wait_ge(kv_done, b + 1)
                act.wait_ge(dec_done, b + 1)
                nc.scalar.activation(tan[:, :, :], gat[:, :, :], ACT.Square).then_inc(sq_done, 1)
                if b >= 1:
                    act.wait_ge(mixed_done, b)
                nc.scalar.activation(o[0][:, :, :], gat[:, :, :], ACT.Copy).then_inc(o_hi, 1)

            def negate(b, i):
                act.wait_ge(top_turned, b + 1)
                if b >= 1:
                    act.wait_ge(neg_stacked, 32 * b)
                nc.scalar.activation(neg[0][:, :], place["turn_max", b, 0][0:2 * H, 0:P], ACT.Copy, scale=-1.0).then_inc(neg_hi, 1)

            def exp(b, i):
                act.wait_ge(shifted_done, HP * b + i + 1)
                if b == 0 and i == 0:
                    act.wait_ge(ffn_w_lo, 6)
                if b >= 1:
                    act.wait_ge(context_done, b)
                    act.wait_ge(sums_done, b)
                nc.scalar.activation(prob[:, 2 * i:2 * i + 2, :, :].rearrange("p h c e -> p (h c) e"),
                                     place["shifted", b, i][:, :, :], ACT.Exp, scale=ATT_SCALE).then_inc(exp_done, 1)

            def x2_high(b, i):
                act.wait_ge(x_turned, b + 1)
                if b >= 1:
                    act.wait_ge(hidden_done, FP * b)
                nc.scalar.activation(x2t[0][:, :, :], place["turn_x", b, 0][:, :].rearrange("p (c t) -> p c t", c=EC),
                                     ACT.Copy).then_inc(x2_hi, 1)

            def gate(b, i):
                n = FP * b + i
                act.wait_ge(hidden_done, n + 1)
                if n >= 2:
                    act.wait_ge(g_lo, n - 1)
                    act.wait_ge(g_hi, n - 1)
                nc.scalar.activation(gu[:, n % 2, :].rearrange("p (k t) -> p k t", k=2),
                                     place["hidden", b, i][:, 0:2, :], ACT.Tanh, scale=0.5).then_inc(gtan, 1)

            def g_high(b, i):
                n = FP * b + i
                act.wait_ge(g_done, n + 1)
                if b >= 1:
                    act.wait_ge(down_done, b)
                nc.scalar.activation(g[0][:, 2 * i:2 * i + 2, :], gu[:, n % 2, :].rearrange("p (k t) -> p k t", k=2),
                                     ACT.Copy).then_inc(g_hi, 1)

            steps = [("mix", 1.4, "low", 1, 0), ("mix", 3.0, "decay", 1, 0), ("mix", 6.8, "query", 1, 0),
                     ("mix", 11.0, "outputs", 1, 0), ("att", 11.0, "negate", 1, 0), ("att", 15.0, "exp", HP, 1.0),
                     ("att", 26.0, "x2", 1, 0), ("ffn", 3.0, "gate", FP, 3.0), ("ffn", 5.0, "g", FP, 3.0)]
            do = {"low": low_high, "decay": decay, "query": query, "outputs": outputs, "negate": negate,
                  "exp": exp, "x2": x2_high, "gate": gate, "g": g_high}
            for kind, b, i in in_order(steps):
                do[kind](b, i)

        @block.vector
        def _(dve):
            nc.vector.memset(quarter[:, :], 0.25)
            nc.vector.memset(ones[:, :], 1.0).then_inc(const_v, 1)

            def split_xt(b, i):
                s = b % 2
                dve.wait_ge(in_xt[s], 16 * (b // 2 + 1))
                if b >= 2:
                    dve.wait_ge(value_done, b - 1)
                nc.vector.tensor_copy(xt[0][:, s, :, :], xt_raw[:, s, :, :]).then_inc(xt_hi, 1)
                dve.wait_ge(xt_hi, b + 1)
                nc.vector.tensor_tensor(xt[1][:, s, :, :], xt_raw[:, s, :, :], xt[0][:, s, :, :], ALU.subtract).then_inc(xt_lo, 1)

            raw_low = raw[:, 0, 0:2 * EC * HD].rearrange("p (w n) -> p w n", w=2)
            low_view = [w[:, :, :, :].rearrange("p w c n -> p w (c n)") for w in w_low]
            dve.wait_ge(in_low, 32)
            nc.vector.tensor_copy(low_view[0], raw_low).then_inc(low_w_hi, 1)
            dve.wait_ge(low_w_hi, 1)
            nc.vector.tensor_tensor(low_view[1], raw_low, low_view[0], ALU.subtract).then_inc(low_w_lo, 1)

            def split_early(b, i):
                if b == 0:
                    dve.wait_ge(v_w_hi, 1)
                    nc.vector.tensor_tensor(w_v[1][:, :, :], raw[:, 2, :].rearrange("p (c n) -> p c n", c=EC),
                                            w_v[0][:, :, :], ALU.subtract).then_inc(v_w_lo, 1)
                    dve.wait_ge(high_w_hi, 1)
                    nc.vector.tensor_tensor(w_high[1][:, :, :], raw[:, 1, :].rearrange("p (w n) -> p w n", w=2),
                                            w_high[0][:, :, :], ALU.subtract).then_inc(high_w_lo, 1)

            def low_rest(b, i):
                ps = place["low", b, 0]
                dve.wait_ge(low_hi, b + 1)
                nc.vector.tensor_tensor(low[1][:, :, :], ps[:, :].rearrange("p (w t) -> p w t", w=2), low[0][:, :, :],
                                        ALU.subtract).then_inc(low_lo, 1)

            def recur(b, i):
                dve.wait_ge(tan2, b + 1)
                if b >= 1:
                    dve.wait_ge(state_done, CC * b)
                    dve.wait_ge(out_done, b)
                nc.vector.tensor_scalar(dec[:, :, :], tan[:, :, :], 0.5, 0.5, ALU.mult, ALU.add).then_inc(dec_done, 1)
                dve.wait_ge(value_done, b + 1)
                nc.vector.scalar_tensor_tensor(out=hid[:, :, :], in0=tan[:, :, :], scalar=1.0, in1=place["value", b, 0][:, :, :],
                                               op0=ALU.subtract, op1=ALU.mult).then_inc(kv_done, 1)
                dve.wait_ge(dec_done, b + 1)
                dve.wait_ge(kv_done, b + 1)
                for cc in range(CC):
                    nc.vector.tensor_tensor_scan(hid[:, cc, :], dec[:, cc, :], hid[:, cc, :], 0.0, ALU.mult,
                                                 ALU.subtract).then_inc(state_done, 1)

            def silu(b, i):
                dve.wait_ge(qtan, b + 1)
                nc.vector.scalar_tensor_tensor(out=gat[:, :, :], in0=gat[:, :, :], scalar=1.0, in1=place["query", b, 0][:, :, :],
                                               op0=ALU.add, op1=ALU.mult).then_inc(silu_done, 1)

            def turn_squares(b, i):
                dve.wait_ge(squares_done, b + 1)
                if b >= 1:
                    dve.wait_ge(ms_done, b)
                nc.vector.transpose(sq_t[:, :, :].rearrange("p t d -> p (t d)"), place["squares", b, 0][:, 0:TT * 32]).then_inc(sq_turned, 1)

            def norm_stats(n, b):
                if b >= 1:
                    dve.wait_ge(mv_done[n], TT * b)
                for t in range(TT):
                    nc.vector.bn_stats(bn[:, n, t, :], res[:, b, t, :]).then_inc(bn_done[n], 1)
                if b >= 1:
                    dve.wait_ge(normed[n], b)
                for t in range(TT):
                    dve.wait_ge(bn_done[n], TT * b + t + 1)
                    nc.vector.bn_aggr(mv[:, n, t, :], bn[:, n, t, :]).then_inc(mv_done[n], 1)

            def norm_apply(n, b):
                dve.wait_ge(rstd_done[n], b + 1)
                for t in range(TT):
                    ins = nc.vector.tensor_scalar(res[:, b, t, :], res[:, b, t, :], mv[:, n, t, 0:1], rstd[:, n, t:t + 1],
                                                  ALU.subtract, ALU.mult)
                ins.then_inc(normed[n], 1)

            def add_mixed(b, i):
                dve.wait_ge(mixed_done, b + 1)
                dve.wait_ge(rms_done, b + 1)
                dve.wait_ge(in_x, 16 * B)
                for t in range(TT):
                    ins = nc.vector.scalar_tensor_tensor(out=res[:, b, t, :], in0=place["mixed", b, 0][:, t * E:(t + 1) * E],
                                                         scalar=rms[:, t:t + 1], in1=res[:, b, t, :],
                                                         op0=ALU.mult, op1=ALU.add)
                ins.then_inc(added[0], 1)
                dve.wait_ge(added[0], b + 1)
                norm_stats(0, b)

            def norm1(b, i):
                norm_apply(0, b)
                dve.wait_ge(normed[0], b + 1)
                if b >= 1:
                    dve.wait_ge(x_stacked, stacks * b)
                nc.vector.tensor_copy(x1_h[0][:, :, :], res[:, b, :, :]).then_inc(x1_hi, 1)
                dve.wait_ge(x1_hi, b + 1)
                nc.vector.tensor_tensor(x1_h[1][:, :, :], res[:, b, :, :], x1_h[0][:, :, :], ALU.subtract).then_inc(x1_lo, 1)

            def maximum(b, i):
                dve.wait_ge(scores_done, HP * b + i + 1)
                if b >= 1:
                    dve.wait_ge(top_turned, b)
                nc.vector.tensor_reduce(top[:, 2 * i:2 * i + 2, :].rearrange("p h c -> p (h c)"),
                                        place["scores", b, i][:, :, :], AX_X, ALU.max).then_inc(top_done, 1)

            def negate_rest(b, i):
                dve.wait_ge(neg_hi, b + 1)
                if b >= 1:
                    dve.wait_ge(neg_stacked, 32 * b)
                nc.vector.scalar_tensor_tensor(out=neg[1][:, :], in0=place["turn_max", b, 0][0:2 * H, 0:P], scalar=-1.0,
                                               in1=neg[0][:, :], op0=ALU.mult, op1=ALU.subtract).then_inc(neg_lo, 1)

            def spread(b, i):
                dve.wait_ge(sums_done, b + 1)
                if b >= 1:
                    dve.wait_ge(inv_done, b)
                nc.vector.transpose(sum_t[:, :, :].rearrange("p a c -> p (a c)"), place["sums", b, 0][:, 0:E]).then_inc(sum_turned, 1)
                dve.wait_ge(sum_turned, b + 1)
                if b >= 1:
                    dve.wait_ge(inv_spread, TT * b)
                nc.vector.reciprocal(inv[:, :, :], sum_t[:, :, :].rearrange("p a (t r) -> p t a r", t=TT)[:, :, :, 0]).then_inc(inv_done, 1)
                dve.wait_ge(inv_done, b + 1)
                if b >= 1:
                    dve.wait_ge(added[1], b)
                for t in range(TT):
                    nc.vector.transpose(inv_b[:, t, :].rearrange("p (a c) -> p a c", c=32),
                                        inv[:, t, :].unsqueeze(2).to_broadcast([P, E // 32, 32])).then_inc(inv_spread, 1)

            def weigh(b, i):
                dve.wait_ge(context_done, b + 1)
                dve.wait_ge(inv_spread, TT * (b + 1))
                nc.vector.tensor_tensor(inv_b[:, :, :], place["context", b, 0][:, :].rearrange("p (t e) -> p t e", t=TT),
                                        inv_b[:, :, :], ALU.mult).then_inc(weighed, 1)
                dve.wait_ge(weighed, b + 1)
                dve.wait_ge(normed[0], b + 1)
                nc.vector.tensor_tensor(res[:, b, :, :], res[:, b, :, :], inv_b[:, :, :], ALU.add).then_inc(added[1], 1)
                dve.wait_ge(added[1], b + 1)
                norm_stats(1, b)

            def norm2(b, i):
                norm_apply(1, b)

            def x2_rest(b, i):
                dve.wait_ge(x2_hi, b + 1)
                nc.vector.tensor_tensor(x2t[1][:, :, :], place["turn_x", b, 0][:, :].rearrange("p (c t) -> p c t", c=EC),
                                        x2t[0][:, :, :], ALU.subtract).then_inc(x2_lo, 1)

            def gate(b, i):
                n = FP * b + i
                ps = place["hidden", b, i]
                v = gu[:, n % 2, :].rearrange("p (k t) -> p k t", k=2)
                dve.wait_ge(gtan, n + 1)
                nc.vector.scalar_tensor_tensor(out=v, in0=v, scalar=1.0, in1=ps[:, 0:2, :], op0=ALU.add,
                                               op1=ALU.mult).then_inc(gate_done, 1)
                dve.wait_ge(gate_done, n + 1)
                nc.vector.tensor_tensor(v, v, ps[:, 2:4, :], ALU.mult).then_inc(g_done, 1)

            def add_down(b, i):
                dve.wait_ge(down_done, b + 1)
                dve.wait_ge(normed[1], b + 1)
                nc.vector.scalar_tensor_tensor(out=res[:, b, :, :], in0=place["down", b, 0][:, :].rearrange("p (t e) -> p t e", t=TT),
                                               scalar=0.5, in1=res[:, b, :, :], op0=ALU.mult, op1=ALU.add).then_inc(added[2], 1)
                dve.wait_ge(added[2], b + 1)
                norm_stats(2, b)

            def norm3(b, i):
                norm_apply(2, b)

            steps = [("mix", 0.0, "xt", 1, 0), ("mix", 0.5, "early", 1, 0), ("mix", 1.7, "low", 1, 0), ("mix", 6.0, "recur", 1, 0),
                     ("mix", 7.0, "silu", 1, 0), ("mix", 14.5, "turn_squares", 1, 0), ("mix", 17.5, "add_mixed", 1, 0),
                     ("mix", 19.0, "norm1", 1, 0), ("att", 6.0, "max", HP, 1.0), ("att", 11.1, "negate", 1, 0),
                     ("att", 20.0, "spread", 1, 0), ("att", 22.0, "weigh", 1, 0), ("att", 24.0, "norm2", 1, 0),
                     ("att", 26.1, "x2", 1, 0), ("ffn", 3.5, "gate", FP, 3.0), ("ffn", 19.0, "add_down", 1, 0),
                     ("ffn", 20.5, "norm3", 1, 0)]
            do = {"xt": split_xt, "early": split_early, "low": low_rest, "recur": recur, "silu": silu, "turn_squares": turn_squares,
                  "add_mixed": add_mixed, "norm1": norm1, "max": maximum, "negate": negate_rest, "spread": spread,
                  "weigh": weigh, "norm2": norm2, "x2": x2_rest, "gate": gate, "add_down": add_down, "norm3": norm3}
            for kind, b, i in in_order(steps):
                do[kind](b, i)

        @block.gpsimd
        def _(pool):
            nc.gpsimd.memset(ident[:, :], 0.0).then_inc(consts, 1)
            nc.gpsimd.memset(power[:, :], -0.5).then_inc(consts, 1)
            pool.wait_ge(consts, 2)
            nc.gpsimd.affine_select(out=ident[:, :], in_=ident[:, :], compare_op=ALU.not_equal, fill=1.0, base=0,
                                    pattern=[[-1, P]], channel_multiplier=1).then_inc(consts, 1)
            nc.gpsimd.memset(pick[:, :, :], 0.0).then_inc(consts, 1)
            pool.wait_ge(consts, 4)
            for t in range(TT):
                nc.gpsimd.memset(pick[:, t, t * D // 2:(t + 1) * D // 2], 1.0).then_inc(consts, 1)
            pool.wait_ge(consts, 6)
            nc.gpsimd.memset(c_stack[STACK:ROWS, :, :].bitcast(F32), 1.0).then_inc(consts, 1)
            pool.wait_ge(consts, 7)

            def same(out, in_):
                return nc.gpsimd.tensor_scalar(out, in_, 1.0, 0.0, ALU.mult, ALU.add)

            def split_ctx(b):
                pool.wait_ge(in_ctx, 16 * (b + 1))
                if b >= 1:
                    pool.wait_ge(ctx_stacked, stacks * b)
                same(ctx_h[0][:, :, :], ctx_raw[:, :, :]).then_inc(ctx_hi, 1)
                pool.wait_ge(ctx_hi, b + 1)
                nc.gpsimd.tensor_tensor(ctx_h[1][:, :, :], ctx_raw[:, :, :], ctx_h[0][:, :, :], ALU.subtract).then_inc(ctx_lo, 1)

            def split_wo():
                pool.wait_ge(in_norm, 16)
                pool.wait_ge(in_o, 16)
                ro = raw[:, 3, :].rearrange("p (c n) -> p c n", c=CC)
                for c in range(CC):
                    nc.gpsimd.tensor_scalar(ro[:, c, :], ro[:, c, :], normw[:, c:c + 1], 1.0, ALU.mult, ALU.mult).then_inc(o_scaled, 1)
                pool.wait_ge(o_scaled, CC)
                same(w_o[0][:, :, :], ro).then_inc(o_w_hi, 1)
                pool.wait_ge(o_w_hi, 1)
                nc.gpsimd.tensor_tensor(w_o[1][:, :, :], ro, w_o[0][:, :, :], ALU.subtract).then_inc(o_w_lo, 1)

            def split_ffn(c):
                pool.wait_ge(in_ffn[c], 16)
                w = (w_gate, w_gate, w_up, w_up, w_down, w_down)[c]
                k = c % 2
                hi, lo = (x[:, k, :] if c < 4 else x[:, 4 * k:4 * k + 4, :].rearrange("p k n -> p (k n)") for x in w)
                same(hi, raw[:, c % 4, :]).then_inc(ffn_w_hi, 1)
                pool.wait_ge(ffn_w_hi, c + 1)
                nc.gpsimd.tensor_tensor(lo, raw[:, c % 4, :], hi, ALU.subtract).then_inc(ffn_w_lo, 1)

            def outputs(b, i):
                pool.wait_ge(silu_done, b + 1)
                pool.wait_ge(state_done, CC * (b + 1))
                nc.gpsimd.tensor_tensor(gat[:, :, :], gat[:, :, :], hid[:, :, :], ALU.mult).then_inc(out_done, 1)
                pool.wait_ge(o_hi, b + 1)
                nc.gpsimd.tensor_tensor(o[1][:, :, :], gat[:, :, :], o[0][:, :, :], ALU.subtract).then_inc(o_lo, 1)

            def inv_root(out, var, factor, eps, ve_, done_ve, done, b):
                nc.gpsimd.tensor_scalar(ve_, var, factor, eps, ALU.mult, ALU.add).then_inc(done_ve, 1)
                pool.wait_ge(done_ve, b + 1)
                nc.gpsimd.tensor_tensor(out, ve_, power[:, :], ALU.pow).then_inc(done, 1)

            def rms_root(b, i):
                pool.wait_ge(sq_turned, b + 1)
                if b >= 1:
                    pool.wait_ge(added[0], b)
                inv_root(rms[:, :], sq_t[:, :, 0], 1.0 / C, 16 * RMS_EPS, ms[:, :], ms_done, rms_done, b)

            def norm_root(n, b):
                pool.wait_ge(mv_done[n], TT * (b + 1))
                if b >= 1:
                    pool.wait_ge(normed[n], b)
                inv_root(rstd[:, n, :], mv[:, n, :, 1], 1.0, LN_EPS, ve[:, n, :], ve_done[n], rstd_done[n], b)

            def g_rest(b, i):
                n = FP * b + i
                pool.wait_ge(g_hi, n + 1)
                nc.gpsimd.tensor_tensor(g[1][:, 2 * i:2 * i + 2, :], gu[:, n % 2, :].rearrange("p (k t) -> p k t", k=2),
                                        g[0][:, 2 * i:2 * i + 2, :], ALU.subtract).then_inc(g_lo, 1)

            def weights(b, i):
                if b == 0:
                    for c in range(2 * i, 2 * i + 2):
                        split_ffn(c)

            split_wo()
            split_ctx(0)
            steps = [("mix", 9.0, "outputs", 1, 0), ("mix", 10.0, "weights", 3, 6), ("mix", 14.8, "rms", 1, 0), ("mix", 18.0, "norm1", 1, 0),
                     ("att", 4.0, "ctx", 1, 0), ("att", 23.0, "norm2", 1, 0), ("ffn", 5.5, "g", FP, 3.0),
                     ("ffn", 20.0, "norm3", 1, 0)]
            do = {"outputs": outputs, "rms": rms_root, "norm1": lambda b, i: norm_root(0, b),
                  "norm2": lambda b, i: norm_root(1, b), "norm3": lambda b, i: norm_root(2, b), "g": g_rest,
                  "weights": weights, "ctx": lambda b, i: split_ctx(b + 1) if b + 1 < B else None}
            for kind, b, i in in_order(steps):
                do[kind](b, i)


def kernel(x, ctx_2048, L0_attn_Wq1, L0_attn_Wq2, L0_attn_Wk1, L0_attn_Wk2, L0_attn_Wv, L0_attn_Wo,
           L0_attn_norm_w, L0_ffn_w_gate, L0_ffn_w_up, L0_ffn_w_down):
    import concourse.bacc as bacc
    import numpy as np
    from concourse.bass_utils import run_bass_kernel_spmd

    a = np.asarray
    arrays = {
        "xT": a(x).transpose(2, 0, 1).reshape(E, B * T),
        "x": a(x),
        "ctx": a(ctx_2048),
        "ctxT": a(ctx_2048).transpose(2, 0, 1).reshape(E, B * T),
        "wq1": a(L0_attn_Wq1), "wq2": a(L0_attn_Wq2), "wk1": a(L0_attn_Wk1), "wk2": a(L0_attn_Wk2),
        "wv": a(L0_attn_Wv), "wo": a(L0_attn_Wo),
        "norm": a(L0_attn_norm_w).reshape(CC, P).T,
        "gateT": a(L0_ffn_w_gate).T, "upT": a(L0_ffn_w_up).T, "downT": a(L0_ffn_w_down).T,
    }
    arrays = {k: np.ascontiguousarray(v) for k, v in arrays.items()}
    nc = bacc.Bacc("TRN2", target_bir_lowering=False, num_devices=1)
    args = [nc.dram_tensor(k, v.shape, F32, kind="ExternalInput").ap() for k, v in arrays.items()]
    out = nc.dram_tensor("out", (B, T, E), F32, kind="ExternalOutput").ap()
    decoder_layer(nc, *args, out)
    r = run_bass_kernel_spmd(nc, [arrays], core_ids=[0])
    return r.results[0]["out"]
```

```python
from contextlib import ExitStack

import concourse.bass as bass
from concourse import mybir

F32 = mybir.dt.float32
F32R = mybir.dt.float32r
ALU = mybir.AluOpType
ACT = mybir.ActivationFunctionType
AX_X = mybir.AxisListType.X

P = 128
B = 4
T = 256
TT = T // P
E = 256
EC = E // P
HD = 128
C = 512
CC = C // P
H = 8
D = T // H
Q = P // D
HP = H // 2
F = 1024
FC = F // P
FP = FC // 2
RMS_EPS = 1e-6
LN_EPS = 1e-5
STACK = 3 * D
WARM_UP = 5
ATT_SCALE = float(D) ** -0.5

PLAN = {
    "sp.w_low": [[0.0]],
    "sp.w_high": [[1.4]],
    "sp.w_v": [[1.9]],
    "sp.w_o": [[4.4]],
    "sp.xt": [[0.5], [0.9], [24.2], [24.7]],
    "sp.ctx": [[8.5], [20.4], [59.0], [64.2]],
    "sp.x": [[23.3], [23.8], [64.7], [65.2]],
    "sp.weights": [[2.4, 2.9, 3.9, 8.0, 9.8, 25.2]],
    "sp.ctx_t": [[22.8], [65.6], [66.1], [88.1]],
    "sp.stack_ctx": [[20.9], [57.0], [74.8], [90.7]],
    "sp.stack_x": [[32.5], [50.6], [77.5], [116.1]],
    "sp.move_x": [[34.5], [52.5], [79.4], [118.5]],
    "sp.store": [[118.0], [151.6], [164.2], [171.8]],
    "pe.low": [[4.9], [6.2], [31.8], [57.0]],
    "pe.decay": [[8.7], [16.5], [51.5], [65.0]],
    "pe.value": [[10.0], [13.8], [52.8], [83.4]],
    "pe.query": [[12.5], [21.9], [55.3], [95.8]],
    "pe.squares": [[21.2], [28.6], [66.7], [103.1]],
    "pe.mixed": [[24.7], [38.2], [68.2], [108.3]],
    "pe.scores": [[37.0, 37.4, 37.8, 42.8], [66.3, 67.4, 67.8, 74.2], [82.6, 83.0, 89.7, 90.1], [120.7, 126.2, 129.2, 134.4]],
    "pe.turn_exp": [[41.0, 44.6, 45.5, 47.6], [70.8, 72.4, 79.8, 80.6], [88.0, 88.8, 97.5, 98.4], [130.2, 132.7, 133.5, 140.0]],
    "pe.inverse": [[48.4], [81.5], [99.3], [140.8]],
    "pe.context": [[49.5], [86.0], [103.8], [141.9]],
    "pe.turn_x": [[56.6], [97.1], [116.0], [149.0]],
    "pe.hidden": [[59.9, 62.4, 74.6, 77.2], [100.5, 105.7, 110.8, 113.4], [118.1, 126.7, 134.8, 137.4], [151.0, 153.6, 156.2, 158.7]],
    "pe.down": [[90.6], [121.1], [143.8], [163.2]],
    "act.w_high": [[5.7]],
    "act.w_v": [[7.1]],
    "act.xt": [[3.5], [4.2], [29.4], [37.5]],
    "act.low": [[6.6], [14.0], [33.3], [58.5]],
    "act.decay": [[10.2], [18.0], [53.0], [66.5]],
    "act.query": [[14.5], [23.3], [59.0], [98.2]],
    "act.outputs": [[20.1], [27.5], [63.1], [101.9]],
    "act.weights": [[8.6, 29.9, 33.8, 34.7, 35.6, 36.6]],
    "act.x1": [[31.1], [49.1], [76.0], [114.7]],
    "act.exp": [[39.0, 40.8, 42.7, 45.6], [68.6, 70.4, 72.2, 76.5], [84.7, 86.5, 91.9, 95.6], [122.7, 128.3, 131.3, 136.5]],
    "act.turned": [[44.5, 47.4, 47.9, 48.6], [74.0, 75.5, 80.8, 81.8], [89.3, 89.9, 99.1, 101.0], [133.1, 133.7, 134.6, 141.2]],
    "act.inverse": [[49.7], [88.8], [100.6], [143.6]],
    "act.x2": [[57.2], [97.7], [116.7], [149.6]],
    "act.gate": [[62.6, 65.2, 78.3, 80.0], [103.8, 108.5, 113.6, 116.2], [120.9, 130.1, 138.3, 140.2], [153.8, 156.4, 158.9, 161.5]],
    "act.g": [[74.5, 75.0, 81.3, 88.3], [109.7, 111.0, 117.4, 121.3], [135.1, 135.6, 140.6, 143.1], [156.8, 159.4, 161.0, 163.6]],
    "dve.w_low": [[2.8]],
    "dve.w_high": [[6.8]],
    "dve.w_v": [[8.5]],
    "dve.turned": [[44.7, 45.6, 47.8, 48.6], [73.1, 76.1, 81.9, 82.5], [89.2, 89.8, 101.8, 102.4], [132.5, 133.7, 136.3, 141.0]],
    "dve.xt": [[4.2], [4.9], [31.0], [49.2]],
    "dve.low": [[7.9], [15.7], [46.9], [59.7]],
    "dve.recur": [[12.4], [20.3], [55.8], [85.9]],
    "dve.silu": [[16.3], [24.8], [60.3], [99.2]],
    "dve.squares": [[24.7], [32.4], [69.8], [104.0]],
    "dve.mixed": [[27.5], [41.6], [71.3], [111.0]],
    "dve.norm1": [[30.4], [46.2], [74.2], [113.9]],
    "dve.x1": [[31.8], [49.8], [76.7], [115.4]],
    "dve.max": [[37.6, 38.9, 40.2, 43.4], [67.2, 68.5, 69.9, 74.8], [83.2, 84.5, 90.4, 94.1], [121.3, 126.8, 129.8, 135.0]],
    "dve.invert": [[47.6], [78.5], [98.9], [140.2]],
    "dve.weigh": [[51.7], [91.8], [105.9], [144.2]],
    "dve.norm2": [[55.1], [95.4], [112.8], [147.6]],
    "dve.x2": [[59.1], [98.3], [117.3], [150.2]],
    "dve.gate": [[63.3, 65.8, 79.0, 80.6], [108.2, 109.6, 116.0, 117.9], [122.6, 131.2, 138.9, 141.6], [154.4, 157.0, 159.5, 162.1]],
    "dve.down": [[96.1], [128.2], [151.5], [168.3]],
    "dve.norm3": [[103.0], [150.8], [163.5], [171.0]],
    "pool.wo": [[13.1]],
    "pool.outputs": [[22.2], [30.3], [65.2], [104.0]],
    "pool.rms": [[25.7], [38.7], [70.1], [109.3]],
    "pool.norm1": [[29.4], [43.5], [73.2], [113.0]],
    "pool.ctx": [[18.4], [55.0], [62.2], [83.2]],
    "pool.norm2": [[54.2], [94.3], [108.4], [146.7]],
    "pool.g": [[75.2, 76.4, 82.0, 89.0], [110.4, 113.9, 118.1, 122.0], [135.8, 137.0, 141.3, 143.8], [157.5, 160.1, 161.7, 164.3]],
    "pool.norm3": [[97.8], [147.6], [158.7], [170.1]],
    "pool.weights": [[20.3, 24.5, 32.6, 33.8, 35.1, 36.3, 37.5, 39.6, 40.8, 42.1, 44.4, 45.6]],
}


def in_order(engine):
    out = []
    for name, starts in PLAN.items():
        if name.split(".")[0] == engine:
            out += [(start, len(out), name.split(".")[1], b, i)
                    for b, parts in enumerate(starts) for i, start in enumerate(parts)]
    return [(name, b, i) for _, _, name, b, i in sorted(out)]


PAIR_KINDS = ("value", "decay", "query", "scores", "turn_exp", "hidden", "down")


def decoder_layer(nc, xT, x, ctx, ctxT, w1, w2, wv, wo, norm, w_ffn, out, x1_dram):
    with ExitStack() as stack:
        def sb(name, shape, dt=F32):
            return stack.enter_context(nc.sbuf_tensor(name, shape, dt))

        def sem(name):
            return stack.enter_context(nc.semaphore(name))

        def halves(name, shape):
            return sb(name + "_hi", shape, F32R), sb(name + "_lo", shape, F32R)

        w_low = halves("w_low", [P, 2, EC, HD])
        w_high = halves("w_high", [P, 2, C])
        w_v = halves("w_v", [P, EC, C])
        w_o = halves("w_o", [P, CC, E])
        w_gate = halves("w_gate", [P, EC, F])
        w_up = halves("w_up", [P, EC, F])
        w_down = halves("w_down", [P, FC, E])
        normw = sb("normw", [P, CC])

        res_i = sb("res_i", [P, 2, TT, E])
        res = sb("res", [P, B, TT, E])
        xt_raw = res[:, :, :, :].rearrange("p b t e -> p b (t e)")
        xt = halves("xt", [P, 2, EC, T])
        low = halves("low", [P, 2, T])
        dec = sb("dec", [P, CC, T])
        hid = sb("hid", [P, CC, T])
        gat = sb("gat", [P, CC, T])
        mix = sb("mix", [P, CC, T])
        o = halves("o", [P, CC, T])
        ctx_raw = sb("ctx_raw", [P, TT, E])
        ctx_h = halves("ctx_h", [P, TT, E])
        x1_h = halves("x1_h", [P, TT, E])
        ctx_t = sb("ctx_t", [P, 2, EC, T])
        c_stack = sb("c_stack", [P, H, E], F32R)
        x_stack = sb("x_stack", [P, H, E], F32R)
        top = sb("top", [P, H, EC])
        shift = sb("shift", [P, H, EC])
        numer = sb("numer", [P, 2, 4, E])
        prob = sb("prob", [P, H, EC, E])
        total = sb("total", [P, H, EC])
        inv = sb("inv", [P, H, EC])
        raw = [prob[:, 2 * s:2 * s + 2, :, :].rearrange("p h c e -> p (h c e)") for s in range(4)]
        raw += [numer[:, s, :, :].rearrange("p h e -> p (h e)") for s in range(2)]
        low_raw = raw[0][:, 0:2 * EC * HD]
        ffn_raw = [raw[s] for s in (4, 5, 0, 1, 2, 3)]
        inv_b = sb("inv_b", [P, TT, E])
        x2t = halves("x2t", [P, EC, T])
        gu = sb("gu", [P, 2, 2 * T])
        g = halves("g", [P, FC, T])
        ident = sb("ident", [P, P])
        ones = sb("ones", [P, D])
        quarter = sb("quarter", [P, 1])
        power = sb("power", [P, TT])
        sq_t = sb("sq_t", [P, TT, 32])
        ms = sb("ms", [P, TT])
        rms = sb("rms", [P, TT])
        bn = sb("bn", [P, 3, TT, 6])
        mv = sb("mv", [P, 3, TT, 2])
        ve = sb("ve", [P, 3, TT])
        rstd = sb("rstd", [P, 3, TT])

        pair = [stack.enter_context(nc.psum_tensor(f"pair{i}", [P, 4, 256], F32)) for i in range(3)]
        single = [stack.enter_context(nc.psum_tensor(f"single{i}", [P, 512], F32)) for i in range(2)]

        in_xt = [sem(f"in_xt{b}") for b in range(B)]
        in_x = [sem("in_x0"), sem("in_x1")]
        in_ctx, in_ctxt = sem("in_ctx"), [sem("in_ctxt0"), sem("in_ctxt1")]
        in_low, in_high, in_v, in_o, in_norm = (sem(n) for n in ("in_low", "in_high", "in_v", "in_o", "in_norm"))
        in_ffn = [sem(f"in_ffn{c}") for c in range(6)]
        low_w_hi, low_w_lo = sem("low_w_hi"), sem("low_w_lo")
        high_w_hi, high_w_lo = sem("high_w_hi"), sem("high_w_lo")
        v_w_hi, v_w_lo = sem("v_w_hi"), sem("v_w_lo")
        o_scaled, o_w_hi, o_w_lo = sem("o_scaled"), sem("o_w_hi"), sem("o_w_lo")
        ffn_w_hi, ffn_w_lo = sem("ffn_w_hi"), sem("ffn_w_lo")
        xt_hi, xt_lo = sem("xt_hi"), sem("xt_lo")
        consts, const_v = sem("consts"), sem("const_v")
        low_done, low_hi, low_lo = sem("low_done"), sem("low_hi"), sem("low_lo")
        value_done, decay_done, query_done = sem("value_done"), sem("decay_done"), sem("query_done")
        tan1, tan2, a_done, kv_done = sem("tan1"), sem("tan2"), sem("a_done"), sem("kv_done")
        state_done, qtan, silu_done, out_done = sem("state_done"), sem("qtan"), sem("silu_done"), sem("out_done")
        sq_done, o_hi, o_lo = sem("sq_done"), sem("o_hi"), sem("o_lo")
        squares_done, sq_turned, ms_done, rms_done = sem("squares_done"), sem("sq_turned"), sem("ms_done"), sem("rms_done")
        mixed_done = sem("mixed_done")
        added = [sem(f"added{n}") for n in range(3)]
        bn_done = [sem(f"bn_done{n}") for n in range(3)]
        mv_done = [sem(f"mv_done{n}") for n in range(3)]
        ve_done = [sem(f"ve_done{n}") for n in range(3)]
        rstd_done = [sem(f"rstd_done{n}") for n in range(3)]
        normed = [sem(f"normed{n}") for n in range(3)]
        ctx_hi, ctx_lo, ctx_stacked = sem("ctx_hi"), sem("ctx_lo"), sem("ctx_stacked")
        x1_hi, x1_lo, x_stacked, x_moved = sem("x1_hi"), sem("x1_lo"), sem("x_stacked"), [sem(f"x_moved{b}") for b in range(B)]
        x_out = sem("x_out")
        scores_done, top_done, shift_done, exp_done = sem("scores_done"), sem("top_done"), sem("shift_done"), sem("exp_done")
        exp_turned, prob_even, prob_odd, context_done = (sem(n) for n in ("exp_turned", "prob_even", "prob_odd", "context_done"))
        inv_done, inv_turned, inv_spread, weighed = sem("inv_done"), sem("inv_turned"), sem("inv_spread"), sem("weighed")
        x_turned, x2_hi, x2_lo = sem("x_turned"), sem("x2_hi"), sem("x2_lo")
        hidden_done, gtan, gate_done, g_done = sem("hidden_done"), sem("gtan"), sem("gate_done"), sem("g_done")
        g_hi, g_lo, down_done = sem("g_hi"), sem("g_lo"), sem("down_done")
        stored = sem("stored")

        freed_by = {"value": [kv_done], "decay": [tan1], "query": [silu_done], "scores": [exp_done],
                    "turn_exp": [prob_even, prob_odd], "hidden": [g_done], "down": [added[2]], "low": [low_lo],
                    "squares": [sq_turned], "mixed": [added[0]], "inverse": [inv_spread], "context": [weighed],
                    "turn_x": [x2_lo]}
        place, before = {}, {}
        for ring, kinds in ((pair, True), (single, False)):
            held = [None] * len(ring)
            n = 0
            for step in in_order("pe"):
                if (step[0] in PAIR_KINDS) == kinds:
                    place[step] = ring[n % len(ring)]
                    before[step] = held[n % len(ring)]
                    held[n % len(ring)] = step
                    n += 1

        def wait_freed(pe, step):
            if before[step] is not None:
                kind, b, i = before[step]
                for read in freed_by[kind]:
                    pe.wait_ge(read, len(PLAN["pe." + kind][b]) * b + i + 1)

        def ffn_chunk(c, first, end):
            w = (w_gate, w_gate, w_up, w_up, w_down, w_down)[c]
            k = c % 2
            if c < 4:
                return [x[:, k, first * E:end * E] for x in w]
            return [x[:, 4 * k + first:4 * k + end, :].rearrange("p k n -> p (k n)") for x in w]

        stacks = 16 * 3

        block = stack.enter_context(nc.Block())

        @block.sync
        def _(sp):
            out_v = out.rearrange("b (t p) e -> b p t e", p=P)

            def load_xt(b):
                sp.dma_start(xt_raw[:, b, :], xT[b]).then_inc(in_xt[b], 16)

            def load_x(b):
                if b >= 2:
                    sp.wait_ge(x_out, 16 * (b - 1))
                    sp.wait_ge(x1_lo, b - 1)
                sp.dma_start(res_i[:, b % 2, :, :].rearrange("p t e -> p (t e)"), x[b]).then_inc(in_x[b % 2], 16)

            def load_ctx(b):
                if b >= 1:
                    sp.wait_ge(ctx_lo, b)
                sp.dma_start(ctx_raw[:, :, :].rearrange("p t e -> p (t e)"), ctx[b]).then_inc(in_ctx, 16)

            def stack_rows(dst, parts, b, done):
                for n, src in enumerate(parts):
                    to = dst[n * D:(n + 1) * D, :, :].rearrange("p (j t) e -> p j (t e)", j=Q)
                    sp.dma_start(to.bitcast(F32), src[:, :, :].rearrange("p t e -> p (t e)").bitcast(F32)).then_inc(done, 16)

            def stack_ctx(b):
                sp.wait_ge(ctx_hi, b + 1)
                sp.wait_ge(ctx_lo, b + 1)
                if b >= 1:
                    sp.wait_ge(scores_done, HP * b)
                stack_rows(c_stack, (ctx_h[0], ctx_h[1], ctx_h[0]), b, ctx_stacked)

            def stack_x(b):
                sp.wait_ge(x1_hi, b + 1)
                sp.wait_ge(x1_lo, b + 1)
                if b >= 1:
                    sp.wait_ge(scores_done, HP * b)
                stack_rows(x_stack, (x1_h[0], x1_h[0], x1_h[1]), b, x_stacked)

            def move_x(b):
                sp.wait_ge(normed[0], b + 1)
                sp.dma_start(x1_dram[b], res_i[:, b % 2, :, :].rearrange("p t e -> p (t e)")).then_inc(x_out, 16)
                sp.wait_ge(x_out, 16 * (b + 1))
                sp.dma_start(res[:, b, :, :].rearrange("p t e -> p (t e)"),
                             x1_dram[b].rearrange("(d j) e -> j d e", j=Q)).then_inc(x_moved[b], 16)

            def load_ffn(c):
                if c >= 2:
                    sp.wait_ge([low_w_lo, high_w_lo, v_w_lo, o_w_lo][c - 2], 1)
                sp.dma_start(ffn_raw[c], w_ffn[:, c, :]).then_inc(in_ffn[c], 16)

            def store(b):
                sp.wait_ge(normed[2], b + 1)
                sp.dma_start(out_v[b], res[:, b, :, :]).then_inc(stored, 16)

            def load_ctx_t(b):
                if b >= 2:
                    sp.wait_ge(context_done, b - 1)
                sp.dma_start(ctx_t[:, b % 2, :, :].rearrange("p c t -> p (c t)"), ctxT[b]).then_inc(in_ctxt[b % 2], 16)

            def load_w_low(b):
                sp.dma_start(low_raw, w1).then_inc(in_low, 16)

            def load_w_high(b):
                sp.dma_start(raw[1], w2).then_inc(in_high, 16)

            def load_w_v(b):
                sp.dma_start(raw[2], wv).then_inc(in_v, 16)

            def load_w_o(b):
                sp.dma_start(normw[:, :], norm).then_inc(in_norm, 16)
                sp.dma_start(raw[3], wo).then_inc(in_o, 16)

            do = {"w_low": load_w_low, "w_high": load_w_high, "w_v": load_w_v, "w_o": load_w_o, "xt": load_xt, "x": load_x, "ctx": load_ctx, "ctx_t": load_ctx_t, "stack_ctx": stack_ctx,
                  "stack_x": stack_x, "move_x": move_x, "store": store}
            for kind, b, i in in_order("sp"):
                if kind == "weights":
                    load_ffn(i)
                else:
                    do[kind](b)
            sp.wait_ge(stored, 16 * B)

        @block.tensor
        def _(pe):
            def product(dst, weights, moving, terms, last=None):
                n = 0
                for term in terms:
                    for wn, xn in ((0, 0), (0, 1), (1, 0)):
                        ins = nc.tensor.matmul(dst, weights[wn](term), moving[xn](term),
                                               start=(n == 0), stop=(n == 3 * len(terms) - 1))
                        n += 1
                return ins

            def low_proj(b, i):
                ps = place["low", b, i]
                pe.wait_ge(low_w_hi, 1)
                pe.wait_ge(low_w_lo, 1)
                pe.wait_ge(xt_hi, b + 1)
                pe.wait_ge(xt_lo, b + 1)
                for w in range(2):
                    ins = product(ps[:, w * T:(w + 1) * T], [lambda c, h=h: w_low[h][:, w, c, :] for h in (0, 1)],
                                  [lambda c, h=h: xt[h][:, b % 2, c, :] for h in (0, 1)], range(EC))
                ins.then_inc(low_done, 1)

            def value_proj(b, i):
                ps = place["value", b, i]
                pe.wait_ge(v_w_hi, 1)
                pe.wait_ge(v_w_lo, 1)
                for cc in range(CC):
                    ins = product(ps[:, cc, :], [lambda c, h=h: w_v[h][:, c, cc * P:(cc + 1) * P] for h in (0, 1)],
                                  [lambda c, h=h: xt[h][:, b % 2, c, :] for h in (0, 1)], range(EC))
                ins.then_inc(value_done, 1)

            def high_proj(kind, b, i):
                ps = place[kind, b, i]
                w, done = (0, query_done) if kind == "query" else (1, decay_done)
                pe.wait_ge(high_w_hi, 1)
                pe.wait_ge(high_w_lo, 1)
                pe.wait_ge(low_hi, b + 1)
                pe.wait_ge(low_lo, b + 1)
                for cc in range(CC):
                    ins = product(ps[:, cc, :], [lambda c, h=h: w_high[h][:, w, cc * P:(cc + 1) * P] for h in (0, 1)],
                                  [lambda c, h=h: low[h][:, w, :] for h in (0, 1)], range(1))
                ins.then_inc(done, 1)

            def squares(b, i):
                ps = place["squares", b, i]
                pe.wait_ge(const_v, 1)
                pe.wait_ge(sq_done, b + 1)
                sq = hid[:, :, :].rearrange("p c (t j d) -> p c t j d", t=TT, j=Q)
                for cc in range(CC):
                    for j in range(Q):
                        ins = nc.tensor.matmul(ps[j * D:(j + 1) * D, 0:TT * D], ones[:, :], sq[:, cc, :, j, :],
                                               start=(cc == 0), stop=(cc == CC - 1))
                ins.then_inc(squares_done, 1)

            def mixed(b, i):
                ps = place["mixed", b, i]
                pe.wait_ge(o_w_hi, 1)
                pe.wait_ge(o_w_lo, 1)
                pe.wait_ge(o_hi, b + 1)
                pe.wait_ge(o_lo, b + 1)
                for t in range(TT):
                    ins = product(ps[:, t * E:(t + 1) * E], [lambda c, h=h: o[h][:, c, t * P:(t + 1) * P] for h in (0, 1)],
                                  [lambda c, h=h: w_o[h][:, c, :] for h in (0, 1)], range(CC))
                ins.then_inc(mixed_done, 1)

            def scores(b, i):
                ps = place["scores", b, i]
                pe.wait_ge(ctx_stacked, stacks * (b + 1))
                pe.wait_ge(x_stacked, stacks * (b + 1))
                for h in range(2):
                    for c in range(EC):
                        ins = nc.tensor.matmul(ps[:, 2 * h + c, :], x_stack[0:STACK, 2 * i + h, c * P:(c + 1) * P],
                                               c_stack[0:STACK, 2 * i + h, :], start=True, stop=True)
                ins.then_inc(scores_done, 1)

            def turn_exp(b, i):
                ps = place["turn_exp", b, i]
                n = HP * b + i
                pe.wait_ge(consts, 3)
                pe.wait_ge(exp_done, n + 1)
                for h in range(2):
                    for k in range(EC):
                        for c in range(EC):
                            ins = nc.tensor.transpose(ps[:, 2 * h + k, c * P:(c + 1) * P],
                                                      numer[:, n % 2, 2 * h + c, k * P:(k + 1) * P], ident[:, :])
                ins.then_inc(exp_turned, 1)

            def inverse(b, i):
                ps = place["inverse", b, i]
                pe.wait_ge(inv_done, b + 1)
                for t in range(TT):
                    for c in range(EC):
                        for j in range(Q):
                            ins = nc.tensor.matmul(ps[j * D:(j + 1) * D, t * E + c * P:t * E + (c + 1) * P],
                                                   inv[:, TT * j + t, c:c + 1].to_broadcast([P, D]), ident[:, :],
                                                   start=True, stop=True)
                ins.then_inc(inv_turned, 1)

            def context(b, i):
                ps = place["context", b, i]
                pe.wait_ge(prob_even, HP * (b + 1))
                pe.wait_ge(prob_odd, HP * (b + 1))
                pe.wait_ge(in_ctxt[b % 2], 16 * (b // 2 + 1))
                for t in range(TT):
                    for c in range(EC):
                        for j in range(Q):
                            first = t * P + j * D
                            ins = nc.tensor.matmul(ps[j * D:(j + 1) * D, t * E:(t + 1) * E],
                                                   ctx_t[:, b % 2, c, first:first + D], prob[:, TT * j + t, c, :],
                                                   start=(c == 0), stop=(c == EC - 1))
                ins.then_inc(context_done, 1)

            def turn_x(b, i):
                ps = place["turn_x", b, i]
                pe.wait_ge(normed[1], b + 1)
                for c in range(EC):
                    for t in range(TT):
                        ins = nc.tensor.transpose(ps[:, c * T + t * P:c * T + (t + 1) * P],
                                                  res[:, b, t, c * P:(c + 1) * P], ident[:, :])
                ins.then_inc(x_turned, 1)

            def hidden(b, i):
                ps = place["hidden", b, i]
                if b == 0 and i == 0:
                    pe.wait_ge(ffn_w_lo, 8)
                pe.wait_ge(x2_hi, b + 1)
                pe.wait_ge(x2_lo, b + 1)
                for n, w in enumerate((w_gate, w_up)):
                    for k in range(2):
                        first = (2 * i + k) * P
                        ins = product(ps[:, 2 * n + k, :], [lambda c, h=h: w[h][:, c, first:first + P] for h in (0, 1)],
                                      [lambda c, h=h: x2t[h][:, c, :] for h in (0, 1)], range(EC))
                ins.then_inc(hidden_done, 1)

            def down(b, i):
                ps = place["down", b, i]
                if b == 0:
                    pe.wait_ge(ffn_w_lo, 12)
                for chunks in (range(FC - 2), range(FC - 2, FC)):
                    ready = FP * b + (chunks[-1] + 1) // 2
                    pe.wait_ge(g_hi, ready)
                    pe.wait_ge(g_lo, ready)
                    for t in range(TT):
                        for c in chunks:
                            for n, (gn, wn) in enumerate(((0, 0), (0, 1), (1, 0))):
                                ins = nc.tensor.matmul(ps[:, 2 * t, :], g[gn][:, c, t * P:(t + 1) * P], w_down[wn][:, c, :],
                                                       start=(c == 0 and n == 0), stop=(c == FC - 1 and n == 2))
                ins.then_inc(down_done, 1)

            pe.wait_ge(const_v, 1)
            for n in range(WARM_UP):
                nc.tensor.matmul(place["low", 0, 0][0:D, 0:E], ones[:, :], gat[:, 0, :], start=True, stop=True)

            do = {"low": low_proj, "value": value_proj, "squares": squares, "mixed": mixed, "scores": scores,
                  "turn_exp": turn_exp, "inverse": inverse, "context": context,
                  "turn_x": turn_x, "hidden": hidden, "down": down,
                  "decay": lambda b, i: high_proj("decay", b, i), "query": lambda b, i: high_proj("query", b, i)}
            for kind, b, i in in_order("pe"):
                wait_freed(pe, (kind, b, i))
                do[kind](b, i)

        @block.scalar
        def _(act):
            def high(hi, raw_, done):
                nc.scalar.activation(hi, raw_, ACT.Copy).then_inc(done, 1)

            def xt_high(b, i):
                s = b % 2
                act.wait_ge(in_xt[b], 16)
                if b >= 2:
                    act.wait_ge(value_done, b - 1)
                    act.wait_ge(low_done, b - 1)
                high(xt[0][:, s, :, :].rearrange("p c t -> p (c t)"), xt_raw[:, b, :], xt_hi)

            def w_high_high(b, i):
                act.wait_ge(in_high, 16)
                high(w_high[0][:, :, :].rearrange("p w n -> p (w n)"), raw[1], high_w_hi)

            def w_v_high(b, i):
                act.wait_ge(in_v, 16)
                high(w_v[0][:, :, :].rearrange("p c n -> p (c n)"), raw[2], v_w_hi)

            def ffn_high(b, i):
                act.wait_ge(in_ffn[i], 16)
                high(ffn_chunk(i, 0, 4)[0], ffn_raw[i], ffn_w_hi)

            def x1_high(b, i):
                act.wait_ge(normed[0], b + 1)
                if b >= 1:
                    act.wait_ge(x_stacked, stacks * b)
                nc.scalar.activation(x1_h[0][:, :, :], res_i[:, b % 2, :, :], ACT.Copy).then_inc(x1_hi, 1)

            def low_high(b, i):
                ps = place["low", b, 0]
                act.wait_ge(low_done, b + 1)
                if b >= 1:
                    act.wait_ge(query_done, b)
                nc.scalar.activation(low[0][:, :, :], ps[:, :].rearrange("p (w t) -> p w t", w=2), ACT.Copy).then_inc(low_hi, 1)

            def decay(b, i):
                ps = place["decay", b, 0]
                act.wait_ge(decay_done, b + 1)
                if b >= 1:
                    act.wait_ge(state_done, CC * b)
                if b == 0:
                    act.wait_ge(const_v, 1)
                nc.scalar.activation(dec[:, :, :], ps[:, :, :], ACT.Tanh, scale=0.5).then_inc(tan1, 1)
                act.wait_ge(tan1, b + 1)
                nc.scalar.activation(dec[:, :, :], dec[:, :, :], ACT.Tanh, bias=quarter[:, 0:1], scale=0.25).then_inc(tan2, 1)

            def query(b, i):
                ps = place["query", b, 0]
                act.wait_ge(query_done, b + 1)
                if b >= 1:
                    act.wait_ge(out_done, b)
                nc.scalar.activation(gat[:, :, :], ps[:, :, :], ACT.Tanh, scale=0.5).then_inc(qtan, 1)

            def outputs(b, i):
                act.wait_ge(out_done, b + 1)
                nc.scalar.activation(hid[:, :, :], mix[:, :, :], ACT.Square).then_inc(sq_done, 1)
                if b >= 1:
                    act.wait_ge(mixed_done, b)
                nc.scalar.activation(o[0][:, :, :], mix[:, :, :], ACT.Copy).then_inc(o_hi, 1)

            def exp(b, i):
                n = HP * b + i
                act.wait_ge(shift_done, n + 1)
                if n < 2:
                    act.wait_ge(ffn_w_lo, 2 * (n + 1))
                if n >= 2:
                    act.wait_ge(exp_turned, n - 1)
                if b >= 1:
                    act.wait_ge(inv_done, b)
                for h in range(2):
                    for c in range(EC):
                        ins = nc.scalar.activation(numer[:, n % 2, 2 * h + c, :], place["scores", b, i][:, 2 * h + c, :], ACT.Exp,
                                                   bias=shift[:, 2 * i + h, c:c + 1], scale=ATT_SCALE,
                                                   accum_out=total[:, 2 * i + h, c:c + 1])
                ins.then_inc(exp_done, 1)

            def keep_turned(b, i):
                act.wait_ge(exp_turned, HP * b + i + 1)
                if b == 0:
                    act.wait_ge(ffn_w_lo, 2 * (i + 3))
                if b >= 1:
                    act.wait_ge(context_done, b)
                nc.scalar.activation(prob[:, 2 * i, :, :], place["turn_exp", b, i][:, 0:2, :], ACT.Copy).then_inc(prob_even, 1)

            def keep_inverse(b, i):
                act.wait_ge(inv_turned, b + 1)
                if b >= 1:
                    act.wait_ge(added[1], b)
                nc.scalar.activation(inv_b[:, :, :], place["inverse", b, 0][:, :].rearrange("p (t e) -> p t e", t=TT),
                                     ACT.Copy).then_inc(inv_spread, 1)

            def x2_high(b, i):
                act.wait_ge(x_turned, b + 1)
                if b >= 1:
                    act.wait_ge(hidden_done, FP * b)
                nc.scalar.activation(x2t[0][:, :, :], place["turn_x", b, 0][:, :].rearrange("p (c t) -> p c t", c=EC),
                                     ACT.Copy).then_inc(x2_hi, 1)

            def gate(b, i):
                n = FP * b + i
                act.wait_ge(hidden_done, n + 1)
                if n >= 2:
                    act.wait_ge(g_lo, n - 1)
                    act.wait_ge(g_hi, n - 1)
                nc.scalar.activation(gu[:, n % 2, :].rearrange("p (k t) -> p k t", k=2),
                                     place["hidden", b, i][:, 0:2, :], ACT.Tanh, scale=0.5).then_inc(gtan, 1)

            def g_high(b, i):
                n = FP * b + i
                act.wait_ge(g_done, n + 1)
                if b >= 1:
                    act.wait_ge(down_done, b)
                nc.scalar.activation(g[0][:, 2 * i:2 * i + 2, :], gu[:, n % 2, :].rearrange("p (k t) -> p k t", k=2),
                                     ACT.Copy).then_inc(g_hi, 1)

            do = {"w_high": w_high_high, "w_v": w_v_high, "xt": xt_high, "x1": x1_high, "low": low_high, "decay": decay, "query": query, "outputs": outputs, "weights": ffn_high,
                  "exp": exp, "turned": keep_turned, "inverse": keep_inverse, "x2": x2_high, "gate": gate, "g": g_high}
            for kind, b, i in in_order("act"):
                do[kind](b, i)

        @block.vector
        def _(dve):
            nc.vector.memset(quarter[:, :], 0.25)
            nc.vector.memset(gat[:, 0, :], 0.0)
            nc.vector.memset(ones[:, :], 1.0).then_inc(const_v, 1)

            def rest(halves_, pattern, raw_, done):
                hi, lo = (x.rearrange(pattern) for x in halves_)
                nc.vector.tensor_tensor(lo, raw_, hi, ALU.subtract).then_inc(done, 1)

            def split_xt(b, i):
                s = b % 2
                dve.wait_ge(xt_hi, b + 1)
                rest([x[:, s, :, :] for x in xt], "p c t -> p (c t)", xt_raw[:, b, :], xt_lo)

            def w_low_both(b, i):
                dve.wait_ge(in_low, 16)
                nc.vector.tensor_copy(w_low[0][:, :, :, :].rearrange("p w c n -> p (w c n)"), low_raw).then_inc(low_w_hi, 1)
                dve.wait_ge(low_w_hi, 1)
                rest([x[:, :, :, :] for x in w_low], "p w c n -> p (w c n)", low_raw, low_w_lo)

            def w_high_rest(b, i):
                dve.wait_ge(high_w_hi, 1)
                rest([x[:, :, :] for x in w_high], "p w n -> p (w n)", raw[1], high_w_lo)

            def w_v_rest(b, i):
                dve.wait_ge(v_w_hi, 1)
                rest([x[:, :, :] for x in w_v], "p c n -> p (c n)", raw[2], v_w_lo)

            def low_rest(b, i):
                ps = place["low", b, 0]
                dve.wait_ge(low_hi, b + 1)
                nc.vector.tensor_tensor(low[1][:, :, :], ps[:, :].rearrange("p (w t) -> p w t", w=2), low[0][:, :, :],
                                        ALU.subtract).then_inc(low_lo, 1)

            def recur(b, i):
                dve.wait_ge(tan2, b + 1)
                nc.vector.tensor_scalar(dec[:, :, :], dec[:, :, :], 0.5, 0.5, ALU.mult, ALU.add).then_inc(a_done, 1)
                dve.wait_ge(a_done, b + 1)
                if b >= 1:
                    dve.wait_ge(squares_done, b)
                dve.wait_ge(value_done, b + 1)
                nc.vector.scalar_tensor_tensor(out=hid[:, :, :], in0=dec[:, :, :], scalar=1.0, in1=place["value", b, 0][:, :, :],
                                               op0=ALU.subtract, op1=ALU.mult).then_inc(kv_done, 1)
                dve.wait_ge(kv_done, b + 1)
                for cc in range(CC):
                    nc.vector.tensor_tensor_scan(hid[:, cc, :], dec[:, cc, :], hid[:, cc, :], 0.0, ALU.mult,
                                                 ALU.subtract).then_inc(state_done, 1)

            def silu(b, i):
                dve.wait_ge(qtan, b + 1)
                nc.vector.scalar_tensor_tensor(out=gat[:, :, :], in0=gat[:, :, :], scalar=1.0, in1=place["query", b, 0][:, :, :],
                                               op0=ALU.add, op1=ALU.mult).then_inc(silu_done, 1)
                dve.wait_ge(silu_done, b + 1)
                dve.wait_ge(state_done, CC * (b + 1))
                if b >= 1:
                    dve.wait_ge(sq_done, b)
                    dve.wait_ge(o_hi, b)
                    dve.wait_ge(o_lo, b)
                for cc in range(CC):
                    ins = nc.vector.tensor_tensor(mix[:, cc, :].rearrange("p (t d j) -> p t j d", t=TT, j=Q),
                                                  gat[:, cc, :].rearrange("p (t j d) -> p t j d", t=TT, j=Q),
                                                  hid[:, cc, :].rearrange("p (t j d) -> p t j d", t=TT, j=Q), ALU.mult)
                ins.then_inc(out_done, 1)

            def turn_squares(b, i):
                dve.wait_ge(squares_done, b + 1)
                if b >= 1:
                    dve.wait_ge(ms_done, b)
                nc.vector.transpose(sq_t[:, :, :].rearrange("p t d -> p (t d)"), place["squares", b, 0][:, 0:TT * 32]).then_inc(sq_turned, 1)

            def norm_stats(n, b, tile):
                if b >= 1:
                    dve.wait_ge(mv_done[n], TT * b)
                for t in range(TT):
                    nc.vector.bn_stats(bn[:, n, t, :], tile[:, t, :]).then_inc(bn_done[n], 1)
                if b >= 1:
                    dve.wait_ge(normed[n], b)
                for t in range(TT):
                    dve.wait_ge(bn_done[n], TT * b + t + 1)
                    nc.vector.bn_aggr(mv[:, n, t, :], bn[:, n, t, :]).then_inc(mv_done[n], 1)

            def norm_apply(n, b, tile):
                dve.wait_ge(rstd_done[n], b + 1)
                for t in range(TT):
                    ins = nc.vector.tensor_scalar(tile[:, t, :], tile[:, t, :], mv[:, n, t, 0:1], rstd[:, n, t:t + 1],
                                                  ALU.subtract, ALU.mult)
                ins.then_inc(normed[n], 1)

            def add_mixed(b, i):
                dve.wait_ge(mixed_done, b + 1)
                dve.wait_ge(rms_done, b + 1)
                dve.wait_ge(in_x[b % 2], 16 * (b // 2 + 1))
                x_i = res_i[:, b % 2, :, :]
                for t in range(TT):
                    ins = nc.vector.scalar_tensor_tensor(out=x_i[:, t, :], in0=place["mixed", b, 0][:, t * E:(t + 1) * E],
                                                         scalar=rms[:, t:t + 1], in1=x_i[:, t, :],
                                                         op0=ALU.mult, op1=ALU.add)
                ins.then_inc(added[0], 1)
                dve.wait_ge(added[0], b + 1)
                norm_stats(0, b, x_i)

            def norm1(b, i):
                x_i = res_i[:, b % 2, :, :]
                norm_apply(0, b, x_i)

            def x1_rest(b, i):
                dve.wait_ge(x1_hi, b + 1)
                nc.vector.tensor_tensor(x1_h[1][:, :, :], res_i[:, b % 2, :, :], x1_h[0][:, :, :], ALU.subtract).then_inc(x1_lo, 1)

            def maximum(b, i):
                n = HP * b + i
                dve.wait_ge(scores_done, n + 1)
                if b >= 1:
                    dve.wait_ge(exp_done, HP * (b - 1) + i + 1)
                tops = top[:, 2 * i:2 * i + 2, :].rearrange("p h c -> p (h c)")
                nc.vector.tensor_reduce(tops, place["scores", b, i][:, :, :], AX_X, ALU.max).then_inc(top_done, 1)
                dve.wait_ge(top_done, n + 1)
                nc.vector.tensor_scalar(shift[:, 2 * i:2 * i + 2, :].rearrange("p h c -> p (h c)"), tops, -ATT_SCALE, 0.0,
                                        ALU.mult, ALU.add).then_inc(shift_done, 1)

            def keep_turned(b, i):
                dve.wait_ge(exp_turned, HP * b + i + 1)
                if b == 0:
                    dve.wait_ge(ffn_w_lo, 2 * (i + 3))
                if b >= 1:
                    dve.wait_ge(context_done, b)
                nc.vector.tensor_copy(prob[:, 2 * i + 1, :, :], place["turn_exp", b, i][:, 2:4, :]).then_inc(prob_odd, 1)

            def invert(b, i):
                dve.wait_ge(exp_done, HP * (b + 1))
                if b >= 1:
                    dve.wait_ge(inv_turned, b)
                nc.vector.reciprocal(inv[:, :, :], total[:, :, :]).then_inc(inv_done, 1)

            def weigh(b, i):
                dve.wait_ge(context_done, b + 1)
                dve.wait_ge(inv_spread, b + 1)
                nc.vector.tensor_tensor(inv_b[:, :, :], place["context", b, 0][:, :].rearrange("p (t e) -> p t e", t=TT),
                                        inv_b[:, :, :], ALU.mult).then_inc(weighed, 1)
                dve.wait_ge(weighed, b + 1)
                dve.wait_ge(x_moved[b], 16)
                nc.vector.tensor_tensor(res[:, b, :, :], res[:, b, :, :], inv_b[:, :, :], ALU.add).then_inc(added[1], 1)
                dve.wait_ge(added[1], b + 1)
                norm_stats(1, b, res[:, b, :, :])

            def norm2(b, i):
                norm_apply(1, b, res[:, b, :, :])

            def x2_rest(b, i):
                dve.wait_ge(x2_hi, b + 1)
                nc.vector.tensor_tensor(x2t[1][:, :, :], place["turn_x", b, 0][:, :].rearrange("p (c t) -> p c t", c=EC),
                                        x2t[0][:, :, :], ALU.subtract).then_inc(x2_lo, 1)

            def gate(b, i):
                n = FP * b + i
                ps = place["hidden", b, i]
                v = gu[:, n % 2, :].rearrange("p (k t) -> p k t", k=2)
                dve.wait_ge(gtan, n + 1)
                nc.vector.scalar_tensor_tensor(out=v, in0=v, scalar=1.0, in1=ps[:, 0:2, :], op0=ALU.add,
                                               op1=ALU.mult).then_inc(gate_done, 1)
                dve.wait_ge(gate_done, n + 1)
                nc.vector.tensor_tensor(v, v, ps[:, 2:4, :], ALU.mult).then_inc(g_done, 1)

            def add_down(b, i):
                dve.wait_ge(down_done, b + 1)
                dve.wait_ge(normed[1], b + 1)
                nc.vector.scalar_tensor_tensor(out=res[:, b, :, :], in0=place["down", b, 0][:, 0:2 * TT:2, :], scalar=0.5,
                                               in1=res[:, b, :, :], op0=ALU.mult, op1=ALU.add).then_inc(added[2], 1)
                dve.wait_ge(added[2], b + 1)
                norm_stats(2, b, res[:, b, :, :])

            def norm3(b, i):
                norm_apply(2, b, res[:, b, :, :])

            do = {"w_low": w_low_both, "w_high": w_high_rest, "w_v": w_v_rest, "xt": split_xt, "low": low_rest, "recur": recur, "silu": silu, "squares": turn_squares,
                  "mixed": add_mixed, "x1": x1_rest, "norm1": norm1, "max": maximum, "turned": keep_turned, "invert": invert,
                  "weigh": weigh, "norm2": norm2, "x2": x2_rest, "gate": gate, "down": add_down, "norm3": norm3}
            for kind, b, i in in_order("dve"):
                do[kind](b, i)

        @block.gpsimd
        def _(pool):
            nc.gpsimd.memset(ident[:, :], 0.0).then_inc(consts, 1)
            nc.gpsimd.memset(power[:, :], -0.5).then_inc(consts, 1)
            pool.wait_ge(consts, 2)
            nc.gpsimd.affine_select(out=ident[:, :], in_=ident[:, :], compare_op=ALU.not_equal, fill=1.0, base=0,
                                    pattern=[[-1, P]], channel_multiplier=1).then_inc(consts, 1)
            pool.wait_ge(consts, 3)

            def same(out, in_):
                return nc.gpsimd.tensor_scalar(out, in_, 1.0, 0.0, ALU.mult, ALU.add)

            def split_ctx(b):
                pool.wait_ge(in_ctx, 16 * (b + 1))
                if b >= 1:
                    pool.wait_ge(ctx_stacked, stacks * b)
                same(ctx_h[0][:, :, :], ctx_raw[:, :, :]).then_inc(ctx_hi, 1)
                pool.wait_ge(ctx_hi, b + 1)
                nc.gpsimd.tensor_tensor(ctx_h[1][:, :, :], ctx_raw[:, :, :], ctx_h[0][:, :, :], ALU.subtract).then_inc(ctx_lo, 1)

            def split_wo():
                pool.wait_ge(in_norm, 16)
                pool.wait_ge(in_o, 16)
                ro = raw[3].rearrange("p (c n) -> p c n", c=CC)
                for c in range(CC):
                    nc.gpsimd.tensor_scalar(ro[:, c, :], ro[:, c, :], normw[:, c:c + 1], 1.0, ALU.mult, ALU.mult).then_inc(o_scaled, 1)
                pool.wait_ge(o_scaled, CC)
                same(w_o[0][:, :, :], ro).then_inc(o_w_hi, 1)
                pool.wait_ge(o_w_hi, 1)
                nc.gpsimd.tensor_tensor(w_o[1][:, :, :], ro, w_o[0][:, :, :], ALU.subtract).then_inc(o_w_lo, 1)

            def ffn_rest(b, i):
                pool.wait_ge(ffn_w_hi, i // 2 + 1)
                first = 2 * (i % 2)
                hi, lo = ffn_chunk(i // 2, first, first + 2)
                nc.gpsimd.tensor_tensor(lo, ffn_raw[i // 2][:, first * E:(first + 2) * E], hi, ALU.subtract).then_inc(ffn_w_lo, 1)

            def outputs(b, i):
                pool.wait_ge(o_hi, b + 1)
                if b >= 1:
                    pool.wait_ge(mixed_done, b)
                nc.gpsimd.tensor_tensor(o[1][:, :, :], mix[:, :, :], o[0][:, :, :], ALU.subtract).then_inc(o_lo, 1)

            def inv_root(out, var, factor, eps, ve_, done_ve, done, b):
                nc.gpsimd.tensor_scalar(ve_, var, factor, eps, ALU.mult, ALU.add).then_inc(done_ve, 1)
                pool.wait_ge(done_ve, b + 1)
                nc.gpsimd.tensor_tensor(out, ve_, power[:, :], ALU.pow).then_inc(done, 1)

            def rms_root(b, i):
                pool.wait_ge(sq_turned, b + 1)
                if b >= 1:
                    pool.wait_ge(added[0], b)
                inv_root(rms[:, :], sq_t[:, :, 0], 1.0 / C, 4 * RMS_EPS, ms[:, :], ms_done, rms_done, b)

            def norm_root(n, b):
                pool.wait_ge(mv_done[n], TT * (b + 1))
                if b >= 1:
                    pool.wait_ge(normed[n], b)
                inv_root(rstd[:, n, :], mv[:, n, :, 1], 1.0, LN_EPS, ve[:, n, :], ve_done[n], rstd_done[n], b)

            def g_rest(b, i):
                n = FP * b + i
                pool.wait_ge(g_hi, n + 1)
                nc.gpsimd.tensor_tensor(g[1][:, 2 * i:2 * i + 2, :], gu[:, n % 2, :].rearrange("p (k t) -> p k t", k=2),
                                        g[0][:, 2 * i:2 * i + 2, :], ALU.subtract).then_inc(g_lo, 1)

            do = {"outputs": outputs, "rms": rms_root, "norm1": lambda b, i: norm_root(0, b),
                  "norm2": lambda b, i: norm_root(1, b), "norm3": lambda b, i: norm_root(2, b), "g": g_rest,
                  "weights": ffn_rest, "wo": lambda b, i: split_wo(), "ctx": lambda b, i: split_ctx(b)}
            for kind, b, i in in_order("pool"):
                do[kind](b, i)


def kernel(x, ctx_2048, L0_attn_Wq1, L0_attn_Wq2, L0_attn_Wk1, L0_attn_Wk2, L0_attn_Wv, L0_attn_Wo,
           L0_attn_norm_w, L0_ffn_w_gate, L0_ffn_w_up, L0_ffn_w_down):
    import concourse.bacc as bacc
    import numpy as np
    from concourse.bass_utils import run_bass_kernel_spmd

    def rows(w):
        return w.reshape(-1, P, w.shape[-1]).transpose(1, 0, 2).reshape(P, -1)

    def channels(z):
        return z.transpose(0, 2, 1).reshape(B, EC, P, T).transpose(0, 2, 1, 3).reshape(B, P, EC * T)

    def interleaved(z):
        return z.reshape(B, TT, Q, D, E).transpose(0, 3, 2, 1, 4).reshape(B, P, TT * E)

    x, c = np.asarray(x), np.asarray(ctx_2048)
    wq1, wk1, wq2, wk2, wv, wo, norm_w, gate, up, down = (np.asarray(w) for w in (
        L0_attn_Wq1, L0_attn_Wk1, L0_attn_Wq2, L0_attn_Wk2, L0_attn_Wv, L0_attn_Wo, L0_attn_norm_w,
        L0_ffn_w_gate, L0_ffn_w_up, L0_ffn_w_down))
    arrays = {
        "xT": channels(x),
        "x": interleaved(x),
        "ctx": interleaved(c),
        "ctxT": channels(c),
        "w1": np.concatenate([rows(wq1), rows(wk1)], axis=1),
        "w2": np.concatenate([wq2, wk2], axis=1),
        "wv": rows(wv),
        "wo": rows(wo),
        "norm": norm_w.reshape(CC, P).T,
        "w_ffn": np.concatenate([rows(gate.T), rows(up.T), rows(down.T)], axis=1).reshape(P, 6, 1024),
    }
    arrays = {k: np.ascontiguousarray(v) for k, v in arrays.items()}
    nc = bacc.Bacc("TRN2", target_bir_lowering=False, num_devices=1)
    args = [nc.dram_tensor(k, v.shape, F32, kind="ExternalInput").ap() for k, v in arrays.items()]
    out = nc.dram_tensor("out", (B, T, E), F32, kind="ExternalOutput").ap()
    x1_dram = nc.dram_tensor("x1_dram", (B, P, TT * E), F32, kind="Internal").ap()
    decoder_layer(nc, *args, out, x1_dram)
    r = run_bass_kernel_spmd(nc, [arrays], core_ids=[0])
    return r.results[0]["out"]
```

```python
from contextlib import ExitStack

from concourse import mybir

F32 = mybir.dt.float32
F32R = mybir.dt.float32r
ALU = mybir.AluOpType
ACT = mybir.ActivationFunctionType
AX_X = mybir.AxisListType.X

P = 128
B = 4
T = 256
TT = T // P
E = 256
EC = E // P
HD = 128
C = 512
CC = C // P
H = 8
D = T // H
Q = P // D
HP = H // 2
F = 1024
FC = F // P
FP = FC // 2
RMS_EPS = 1e-6
LN_EPS = 1e-5
STACK = 3 * D
WARM_UP = 4
ATT_SCALE = float(D) ** -0.5

PLAN = {
    "sp.w_low": [[0.6]],
    "sp.w_high": [[1.17, 1.52]],
    "sp.w_v": [[2.9]],
    "sp.w_o": [[3.47]],
    "sp.xt": [[1.0], [2.5], [4.49], [9.3]],
    "sp.ctx": [[3.4], [13.9], [28.23], [62.1]],
    "sp.x": [[5.35], [16.12], [37.33], [65.77]],
    "sp.weights": [[5.3, 5.8, 6.3, 10.3, 10.39, 37.9]],
    "sp.ctx_t": [[5.21], [11.77], [67.9], [72.28]],
    "sp.stack_ctx": [[10.5], [44.41], [59.63], [81.02]],
    "sp.stack_x": [[29.94], [44.42], [65.77], [87.37]],
    "sp.move_x": [[33.7], [49.3], [65.92], [89.74]],
    "sp.store": [[94.5], [116.99], [133.45], [148.52]],
    "pe.low": [[4.7, 5.7], [8.4, 9.0], [20.7, 21.3], [28.84, 31.0]],
    "pe.decay": [[6.4, 7.7], [14.1, 14.8], [24.5, 25.2], [33.88, 35.2]],
    "pe.value": [[10.1, 12.7], [16.88, 17.4], [25.9, 27.2], [35.9, 40.98]],
    "pe.query": [[12.09, 12.1], [18.81, 20.0], [28.44, 30.89], [44.76, 45.3]],
    "pe.squares": [[18.09], [28.4], [40.02], [61.7]],
    "pe.mixed": [[23.4], [32.78], [45.93], [73.8]],
    "pe.scores": [[37.2, 37.9, 43.6, 44.8], [52.8, 54.4, 54.46, 59.1], [69.77, 70.27, 77.5, 82.58], [96.3, 98.7, 106.6, 106.93]],
    "pe.turn_exp": [[42.8, 48.68, 49.8, 51.08], [57.9, 60.9, 63.0, 63.9], [76.73, 77.2, 84.91, 92.16], [102.63, 105.1, 110.72, 114.0]],
    "pe.inverse": [[54.0], [67.92], [95.21], [115.61]],
    "pe.context": [[55.45], [71.3], [96.7], [118.17]],
    "pe.turn_x": [[62.4], [84.24], [106.56], [128.0]],
    "pe.hidden": [[64.8, 67.89, 80.01, 82.05], [89.4, 93.3, 101.18, 101.7], [114.83, 118.86, 122.1, 122.3], [132.8, 135.99, 137.21, 140.5]],
    "pe.down": [[84.61], [107.8], [131.88], [140.65]],
    "act.w_high": [[4.15, 5.5]],
    "act.w_v": [[7.32]],
    "act.xt": [[4.0], [6.3], [14.9], [21.3]],
    "act.low": [[6.49, 6.8], [11.12, 13.2], [23.8, 24.0], [30.58, 32.1]],
    "act.decay": [[8.6, 11.51], [16.82, 19.4], [25.4, 26.3], [35.63, 36.59]],
    "act.query": [[12.7, 13.5], [19.5, 23.38], [30.3, 31.6], [47.25, 48.1]],
    "act.outputs": [[17.3, 18.4], [24.4, 26.29], [34.2, 39.11], [51.8, 53.8]],
    "act.weights": [[14.0, 22.8, 32.3, 33.96, 46.18, 48.6]],
    "act.x1": [[30.8], [45.85], [64.7], [90.04]],
    "act.exp": [[41.73, 43.1, 47.75, 51.03], [55.59, 59.41, 60.0, 61.9], [72.32, 73.4, 79.6, 87.5], [101.44, 103.71, 110.36, 110.9]],
    "act.turned": [[43.9, 51.39, 52.8, 53.3], [61.58, 64.2, 65.2, 67.46], [74.23, 77.8, 89.34, 91.54], [105.3, 107.3, 113.29, 116.52]],
    "act.inverse": [[56.28], [71.0], [99.28], [117.32]],
    "act.x2": [[64.17], [87.09], [107.5], [130.12]],
    "act.gate": [[65.51, 70.2, 79.77, 83.2], [91.23, 96.1, 101.9, 104.4], [117.4, 122.3, 125.5, 126.09], [130.5, 140.15, 140.8, 143.3]],
    "act.g": [[76.36, 79.09, 83.8, 84.25], [93.97, 101.29, 105.57, 106.5], [123.81, 124.9, 127.07, 129.5], [138.01, 140.67, 143.54, 145.4]],
    "dve.w_low": [[-2.34]],
    "dve.w_high": [[5.08, 8.37]],
    "dve.w_v": [[8.8]],
    "dve.turned": [[43.29, 50.4, 53.0, 54.7], [62.2, 62.41, 66.94, 68.46], [77.41, 79.2, 89.71, 94.95], [106.4, 107.0, 115.11, 115.95]],
    "dve.xt": [[4.7], [], [], []],
    "dve.low": [[6.14, 7.98], [10.3, 13.6], [24.3, 27.8], [31.76, 34.0]],
    "dve.recur": [[12.78, 18.82], [20.59, 21.5], [29.31, 34.08], [40.6, 40.99]],
    "dve.silu": [[14.82, 19.54], [23.24, 24.6], [29.33, 35.1], [47.5, 49.0]],
    "dve.squares": [[21.0], [34.97], [48.9], [64.23]],
    "dve.mixed": [[28.17], [35.26], [50.72], [79.8]],
    "dve.norm1": [[28.9], [42.57], [63.9], [88.25]],
    "dve.x1": [[30.28], [45.81], [65.4], [91.6]],
    "dve.max": [[38.3, 39.5, 45.06, 46.88], [53.6, 55.3, 55.65, 60.4], [69.02, 71.7, 78.1, 82.79], [98.0, 98.65, 107.6, 109.22]],
    "dve.invert": [[52.61], [66.0], [94.46], [113.4]],
    "dve.weigh": [[58.1], [74.2], [100.4], [120.5]],
    "dve.norm2": [[61.5], [81.36], [104.2], [126.03]],
    "dve.x2": [[64.4], [87.36], [113.34], [132.0]],
    "dve.gate": [[68.2, 72.9, 82.15, 83.15], [94.07, 96.7, 102.8, 105.67], [120.85, 125.22, 126.2, 129.06], [137.42, 138.8, 140.08, 142.1]],
    "dve.down": [[89.2], [114.16], [133.0], [148.3]],
    "dve.norm3": [[95.5], [118.2], [135.7], [151.0]],
    "dve.g": [[], [], [], [None, None, None, 145.58]],
    "pool.xt": [[], [7.6], [17.3], [27.57]],
    "pool.shift": [[37.72, 40.8, 45.21, 48.54], [54.9, 56.6, 57.96, 61.7], [73.48, 75.56, 77.56, 88.9], [100.43, 100.7, 108.9, 110.0]],
    "pool.widen": [[54.61], [65.98], [92.09], [113.16]],
    "pool.wo": [[10.7]],
    "pool.outputs": [[18.5, 19.06], [28.8, 30.1], [41.31, 42.1], [61.9, 64.96]],
    "pool.rms": [[21.3], [33.33], [48.82], [64.3]],
    "pool.norm1": [[28.38], [38.95], [55.0], [84.92]],
    "pool.ctx": [[8.5], [21.87], [56.71], [63.24]],
    "pool.norm2": [[60.6], [80.3], [105.95], [122.2]],
    "pool.g": [[76.66, 81.7, 84.5, 90.55], [99.5, 100.77, 109.42, 112.2], [122.07, 127.17, 128.19, 133.18], [137.77, 139.26, 141.36]],
    "pool.norm3": [[91.0], [117.6], [134.8], [147.94]],
    "pool.weights": [[16.1, 27.63, 31.3, 32.5, 33.18, 37.32, 40.62, 44.6, 46.1, 48.25, 50.1, 51.3]],
}


def in_order(engine):
    out = []
    for name, starts in PLAN.items():
        if name.split(".")[0] == engine:
            out += [(start, len(out), name.split(".")[1], b, i)
                    for b, parts in enumerate(starts) for i, start in enumerate(parts) if start is not None]
    return [(name, b, i) for _, _, name, b, i in sorted(out)]


PAIR_KINDS = ("low", "value", "decay", "query", "scores", "turn_exp", "hidden", "down")

HALVED = ("low", "value", "decay", "query")


def half(i):
    return range(i * CC // 2, (i + 1) * CC // 2)


def decoder_layer(nc, xT, x, ctx, ctxT, w1, w2, wv, wo, norm, w_ffn, out, x1_dram):
    with ExitStack() as stack:
        def sb(name, shape, dt=F32):
            return stack.enter_context(nc.sbuf_tensor(name, shape, dt))

        def sem(name):
            return stack.enter_context(nc.semaphore(name))

        def halves(name, shape):
            return sb(name + "_hi", shape, F32R), sb(name + "_lo", shape, F32R)

        w_low = halves("w_low", [P, 2, EC, HD])
        w_high = halves("w_high", [P, 2, C])
        w_v = halves("w_v", [P, EC, C])
        w_o = halves("w_o", [P, CC, E])
        w_gate = halves("w_gate", [P, EC, F])
        w_up = halves("w_up", [P, EC, F])
        w_down = halves("w_down", [P, FC, E])
        normw = sb("normw", [P, CC])

        res_i = sb("res_i", [P, 2, TT, E])
        res = sb("res", [P, B, TT, E])
        xt_raw = res[:, :, :, :].rearrange("p b t e -> p b (t e)")
        xt = halves("xt", [P, 2, EC, T])
        low = halves("low", [P, 2, T])
        dec = sb("dec", [P, CC, T])
        hid = sb("hid", [P, CC, T])
        gat = sb("gat", [P, CC, T])
        mix = sb("mix", [P, CC, T])
        o = halves("o", [P, CC, T])
        ctx_raw = sb("ctx_raw", [P, TT, E])
        ctx_h = halves("ctx_h", [P, TT, E])
        x1_h = halves("x1_h", [P, TT, E])
        ctx_t = sb("ctx_t", [P, 2, EC, T])
        c_stack = sb("c_stack", [P, H, E], F32R)
        x_stack = sb("x_stack", [P, H, E], F32R)
        top = sb("top", [P, H, EC])
        shift = sb("shift", [P, H, EC])
        numer = sb("numer", [P, 2, 4, E])
        prob = sb("prob", [P, H, EC, E])
        total = sb("total", [P, H, EC])
        inv = sb("inv", [P, H, EC])
        inv_wide = sb("inv_wide", [P, TT, EC, Q, D])
        raw = [prob[:, 2 * s:2 * s + 2, :, :].rearrange("p h c e -> p (h c e)") for s in range(4)]
        raw += [numer[:, s, :, :].rearrange("p h e -> p (h e)") for s in range(2)]
        low_raw = raw[0][:, 0:2 * EC * HD]
        ffn_raw = [raw[s] for s in (4, 5, 0, 1, 2, 3)]
        inv_b = sb("inv_b", [P, TT, E])
        x2t = halves("x2t", [P, EC, T])
        gu = sb("gu", [P, 2, 2 * T])
        g = halves("g", [P, FC, T])
        ident = sb("ident", [P, P])
        ones = sb("ones", [P, D])
        quarter = sb("quarter", [P, 1])
        power = sb("power", [P, TT])
        sq_t = sb("sq_t", [P, TT, 32])
        ms = sb("ms", [P, TT])
        rms = sb("rms", [P, TT])
        bn = sb("bn", [P, 3, TT, 6])
        mv = sb("mv", [P, 3, TT, 2])
        ve = sb("ve", [P, 3, TT])
        rstd = sb("rstd", [P, 3, TT])

        pair = [stack.enter_context(nc.psum_tensor(f"pair{i}", [P, 4, 256], F32)) for i in range(3)]
        single = [stack.enter_context(nc.psum_tensor(f"single{i}", [P, 512], F32)) for i in range(2)]

        in_xt = [sem(f"in_xt{b}") for b in range(B)]
        in_x = [sem("in_x0"), sem("in_x1")]
        in_ctx, in_ctxt = sem("in_ctx"), [sem("in_ctxt0"), sem("in_ctxt1")]
        in_low, in_v, in_o, in_norm = (sem(n) for n in ("in_low", "in_v", "in_o", "in_norm"))
        in_high = [sem("in_high0"), sem("in_high1")]
        in_ffn = [sem(f"in_ffn{c}") for c in range(6)]
        low_w_hi, low_w_lo = sem("low_w_hi"), sem("low_w_lo")
        high_w_hi, high_w_lo = sem("high_w_hi"), sem("high_w_lo")
        v_w_hi, v_w_lo = sem("v_w_hi"), sem("v_w_lo")
        o_scaled, o_w_hi, o_w_lo = sem("o_scaled"), sem("o_w_hi"), sem("o_w_lo")
        ffn_w_hi, ffn_w_lo = sem("ffn_w_hi"), sem("ffn_w_lo")
        xt_hi, xt_lo = sem("xt_hi"), sem("xt_lo")
        consts, const_v = sem("consts"), sem("const_v")
        low_done, low_hi, low_lo = sem("low_done"), sem("low_hi"), sem("low_lo")
        value_done, decay_done, query_done = sem("value_done"), sem("decay_done"), sem("query_done")
        tan1, tan2, a_done, kv_done = sem("tan1"), sem("tan2"), sem("a_done"), sem("kv_done")
        state_done, qtan, silu_done, out_done = sem("state_done"), sem("qtan"), sem("silu_done"), sem("out_done")
        sq_done, o_hi, o_lo = sem("sq_done"), sem("o_hi"), sem("o_lo")
        squares_done, sq_turned, ms_done, rms_done = sem("squares_done"), sem("sq_turned"), sem("ms_done"), sem("rms_done")
        mixed_done = sem("mixed_done")
        added = [sem(f"added{n}") for n in range(3)]
        bn_done = [sem(f"bn_done{n}") for n in range(3)]
        mv_done = [sem(f"mv_done{n}") for n in range(3)]
        ve_done = [sem(f"ve_done{n}") for n in range(3)]
        rstd_done = [sem(f"rstd_done{n}") for n in range(3)]
        normed = [sem(f"normed{n}") for n in range(3)]
        ctx_hi, ctx_lo, ctx_stacked = sem("ctx_hi"), sem("ctx_lo"), sem("ctx_stacked")
        x1_hi, x1_lo, x_stacked, x_moved = sem("x1_hi"), sem("x1_lo"), sem("x_stacked"), [sem(f"x_moved{b}") for b in range(B)]
        x_out = sem("x_out")
        scores_done, top_done, shift_done, exp_done = sem("scores_done"), sem("top_done"), sem("shift_done"), sem("exp_done")
        exp_turned, prob_even, prob_odd, context_done = (sem(n) for n in ("exp_turned", "prob_even", "prob_odd", "context_done"))
        inv_widened, inv_done, inv_turned, inv_spread, weighed = sem("inv_widened"), sem("inv_done"), sem("inv_turned"), sem("inv_spread"), sem("weighed")
        x_turned, x2_hi, x2_lo = sem("x_turned"), sem("x2_hi"), sem("x2_lo")
        hidden_done, gtan, gate_done, g_done = sem("hidden_done"), sem("gtan"), sem("gate_done"), sem("g_done")
        g_hi, g_lo, down_done = sem("g_hi"), sem("g_lo"), sem("down_done")
        stored = sem("stored")

        freed_by = {"value": [kv_done], "decay": [tan1], "query": [silu_done], "scores": [exp_done],
                    "turn_exp": [prob_even, prob_odd], "hidden": [g_done], "down": [added[2]], "low": [low_lo],
                    "squares": [sq_turned], "mixed": [added[0]], "inverse": [inv_spread], "context": [weighed],
                    "turn_x": [x2_lo]}
        place, before = {}, {}
        for ring, kinds in ((pair, True), (single, False)):
            held = [None] * len(ring)
            n = 0
            for step in in_order("pe"):
                if step[0] in HALVED and step[2] > 0:
                    before[step] = None
                elif (step[0] in PAIR_KINDS) == kinds:
                    place[step] = ring[n % len(ring)]
                    before[step] = held[n % len(ring)]
                    held[n % len(ring)] = step
                    n += 1

        def wait_freed(pe, step):
            if before[step] is not None:
                kind, b, i = before[step]
                if kind in HALVED:
                    i = 1
                for read in freed_by[kind]:
                    pe.wait_ge(read, len(PLAN["pe." + kind][b]) * b + i + 1)

        def ffn_chunk(c, first, end):
            w = (w_gate, w_gate, w_up, w_up, w_down, w_down)[c]
            k = c % 2
            if c < 4:
                return [x[:, k, first * E:end * E] for x in w]
            return [x[:, 4 * k + first:4 * k + end, :].rearrange("p k n -> p (k n)") for x in w]

        stacks = 16 * 3

        block = stack.enter_context(nc.Block())

        @block.sync
        def _(sp):
            out_v = out.rearrange("b (t p) e -> b p t e", p=P)

            def load_xt(b):
                sp.dma_start(xt_raw[:, b, :], xT[b]).then_inc(in_xt[b], 16)

            def load_x(b):
                if b >= 2:
                    sp.wait_ge(x_out, 16 * (b - 1))
                    sp.wait_ge(x1_lo, b - 1)
                sp.dma_start(res_i[:, b % 2, :, :].rearrange("p t e -> p (t e)"), x[b]).then_inc(in_x[b % 2], 16)

            def load_ctx(b):
                if b >= 1:
                    sp.wait_ge(ctx_lo, b)
                sp.dma_start(ctx_raw[:, :, :].rearrange("p t e -> p (t e)"), ctx[b]).then_inc(in_ctx, 16)

            def stack_rows(dst, parts, done):
                for n, src, ready in parts:
                    sp.wait_ge(*ready)
                    to = dst[n * D:(n + 1) * D, :, :].rearrange("p (j t) e -> p j (t e)", j=Q)
                    sp.dma_start(to.bitcast(F32), src[:, :, :].rearrange("p t e -> p (t e)").bitcast(F32)).then_inc(done, 16)

            def stack_ctx(b):
                if b >= 1:
                    sp.wait_ge(scores_done, HP * b)
                hi, lo = (ctx_hi, b + 1), (ctx_lo, b + 1)
                stack_rows(c_stack, ((0, ctx_h[0], hi), (2, ctx_h[0], hi), (1, ctx_h[1], lo)), ctx_stacked)

            def stack_x(b):
                if b >= 1:
                    sp.wait_ge(scores_done, HP * b)
                hi, lo = (x1_hi, b + 1), (x1_lo, b + 1)
                stack_rows(x_stack, ((0, x1_h[0], hi), (1, x1_h[0], hi), (2, x1_h[1], lo)), x_stacked)

            def move_x(b):
                sp.wait_ge(normed[0], b + 1)
                sp.dma_start(x1_dram[b], res_i[:, b % 2, :, :].rearrange("p t e -> p (t e)")).then_inc(x_out, 16)
                sp.wait_ge(x_out, 16 * (b + 1))
                sp.dma_start(res[:, b, :, :].rearrange("p t e -> p (t e)"),
                             x1_dram[b].rearrange("(d j) e -> j d e", j=Q)).then_inc(x_moved[b], 16)

            def load_ffn(c):
                if c >= 2:
                    sp.wait_ge([low_w_lo, high_w_lo, v_w_lo, o_w_lo][c - 2], 2 if c == 3 else 1)
                sp.dma_start(ffn_raw[c], w_ffn[:, c, :]).then_inc(in_ffn[c], 16)

            def store(b):
                sp.wait_ge(normed[2], b + 1)
                sp.dma_start(out_v[b], res[:, b, :, :]).then_inc(stored, 16)

            def load_ctx_t(b):
                if b >= 2:
                    sp.wait_ge(context_done, b - 1)
                sp.dma_start(ctx_t[:, b % 2, :, :].rearrange("p c t -> p (c t)"), ctxT[b]).then_inc(in_ctxt[b % 2], 16)

            def load_w_low(b):
                sp.dma_start(low_raw, w1).then_inc(in_low, 16)

            def load_w_high(b, i):
                cols = slice((1 - i) * C, (2 - i) * C)
                sp.dma_start(raw[1][:, cols], w2[:, cols]).then_inc(in_high[i], 16)

            def load_w_v(b):
                sp.dma_start(raw[2], wv).then_inc(in_v, 16)

            def load_w_o(b):
                sp.dma_start(normw[:, :], norm).then_inc(in_norm, 16)
                sp.dma_start(raw[3], wo).then_inc(in_o, 16)

            do = {"w_low": load_w_low, "w_v": load_w_v, "w_o": load_w_o, "xt": load_xt, "x": load_x,
                  "ctx": load_ctx, "ctx_t": load_ctx_t, "stack_ctx": stack_ctx, "stack_x": stack_x, "move_x": move_x, "store": store}
            for kind, b, i in in_order("sp"):
                if kind == "weights":
                    load_ffn(i)
                elif kind == "w_high":
                    load_w_high(b, i)
                else:
                    do[kind](b)
            sp.wait_ge(stored, 16 * B)

        @block.tensor
        def _(pe):
            MOVING_LAST = ((0, 0), (1, 0), (0, 1))
            WEIGHTS_LAST = ((0, 0), (0, 1), (1, 0))

            def product(dst, weights, moving, terms, passes, lower, ready):
                n = 0
                for wn, xn in passes:
                    if (wn, xn) == passes[-1]:
                        pe.wait_ge(lower, ready)
                    for term in terms:
                        ins = nc.tensor.matmul(dst, weights[wn](term), moving[xn](term),
                                               start=(n == 0), stop=(n == 3 * len(terms) - 1))
                        n += 1
                return ins

            def low_proj(b, i):
                ps = place["low", b, 0]
                w = 1 - i
                pe.wait_ge(low_w_hi, 1)
                pe.wait_ge(low_w_lo, 1)
                pe.wait_ge(xt_hi, b + 1)
                product(ps[:, 2 * w, :], [lambda c, h=h: w_low[h][:, w, c, :] for h in (0, 1)],
                        [lambda c, h=h: xt[h][:, b % 2, c, :] for h in (0, 1)], range(EC),
                        MOVING_LAST, xt_lo, b + 1).then_inc(low_done, 1)

            def value_proj(b, i):
                ps = place["value", b, 0]
                pe.wait_ge(v_w_hi, 1)
                pe.wait_ge(v_w_lo, 1)
                for cc in half(i):
                    ins = product(ps[:, cc, :], [lambda c, h=h: w_v[h][:, c, cc * P:(cc + 1) * P] for h in (0, 1)],
                                  [lambda c, h=h: xt[h][:, b % 2, c, :] for h in (0, 1)], range(EC),
                                  MOVING_LAST, xt_lo, b + 1)
                ins.then_inc(value_done, 1)

            def high_proj(kind, b, i):
                ps = place[kind, b, 0]
                w, done = (0, query_done) if kind == "query" else (1, decay_done)
                pe.wait_ge(high_w_hi, 2 - w)
                pe.wait_ge(high_w_lo, 2 - w)
                pe.wait_ge(low_hi, 2 * b + 2 - w)
                for cc in half(i):
                    ins = product(ps[:, cc, :], [lambda c, h=h: w_high[h][:, w, cc * P:(cc + 1) * P] for h in (0, 1)],
                                  [lambda c, h=h: low[h][:, w, :] for h in (0, 1)], range(1),
                                  MOVING_LAST, low_lo, 2 * b + 2 - w)
                ins.then_inc(done, 1)

            def squares(b, i):
                ps = place["squares", b, i]
                pe.wait_ge(const_v, 1)
                sq = hid[:, :, :].rearrange("p c (t j d) -> p c t j d", t=TT, j=Q)
                for cc in range(CC):
                    pe.wait_ge(sq_done, 2 * b + 1 + cc // 2)
                    for j in range(Q):
                        ins = nc.tensor.matmul(ps[j * D:(j + 1) * D, 0:TT * D], ones[:, :], sq[:, cc, :, j, :],
                                               start=(cc == 0), stop=(cc == CC - 1))
                ins.then_inc(squares_done, 1)

            def mixed(b, i):
                ps = place["mixed", b, i]
                pe.wait_ge(o_w_hi, 1)
                pe.wait_ge(o_w_lo, 1)
                pe.wait_ge(o_hi, 2 * (b + 1))
                for t in range(TT):
                    ins = product(ps[:, t * E:(t + 1) * E], [lambda c, h=h: o[h][:, c, t * P:(t + 1) * P] for h in (0, 1)],
                                  [lambda c, h=h: w_o[h][:, c, :] for h in (0, 1)], range(CC),
                                  WEIGHTS_LAST, o_lo, 2 * (b + 1))
                ins.then_inc(mixed_done, 1)

            def scores(b, i):
                ps = place["scores", b, i]
                pe.wait_ge(ctx_stacked, stacks * (b + 1))
                pe.wait_ge(x_stacked, stacks * (b + 1))
                for h in range(2):
                    for c in range(EC):
                        ins = nc.tensor.matmul(ps[:, 2 * h + c, :], x_stack[0:STACK, 2 * i + h, c * P:(c + 1) * P],
                                               c_stack[0:STACK, 2 * i + h, :], start=True, stop=True)
                ins.then_inc(scores_done, 1)

            def turn_exp(b, i):
                ps = place["turn_exp", b, i]
                n = HP * b + i
                pe.wait_ge(consts, 3)
                pe.wait_ge(exp_done, n + 1)
                for h in range(2):
                    for k in range(EC):
                        for c in range(EC):
                            ins = nc.tensor.transpose(ps[:, 2 * h + k, c * P:(c + 1) * P],
                                                      numer[:, n % 2, 2 * h + c, k * P:(k + 1) * P], ident[:, :])
                ins.then_inc(exp_turned, 1)

            def inverse(b, i):
                ps = place["inverse", b, i]
                pe.wait_ge(inv_widened, b + 1)
                for t in range(TT):
                    for c in range(EC):
                        ins = nc.tensor.transpose(ps[:, t * E + c * P:t * E + (c + 1) * P],
                                                  inv_wide[:, t, c, :, :].rearrange("p j d -> p (j d)"), ident[:, :])
                ins.then_inc(inv_turned, 1)

            def context(b, i):
                ps = place["context", b, i]
                pe.wait_ge(prob_even, HP * (b + 1))
                pe.wait_ge(prob_odd, HP * (b + 1))
                pe.wait_ge(in_ctxt[b % 2], 16 * (b // 2 + 1))
                for t in range(TT):
                    for c in range(EC):
                        for j in range(Q):
                            first = t * P + j * D
                            ins = nc.tensor.matmul(ps[j * D:(j + 1) * D, t * E:(t + 1) * E],
                                                   ctx_t[:, b % 2, c, first:first + D], prob[:, TT * j + t, c, :],
                                                   start=(c == 0), stop=(c == EC - 1))
                ins.then_inc(context_done, 1)

            def turn_x(b, i):
                ps = place["turn_x", b, i]
                pe.wait_ge(normed[1], b + 1)
                for c in range(EC):
                    for t in range(TT):
                        ins = nc.tensor.transpose(ps[:, c * T + t * P:c * T + (t + 1) * P],
                                                  res[:, b, t, c * P:(c + 1) * P], ident[:, :])
                ins.then_inc(x_turned, 1)

            def hidden(b, i):
                ps = place["hidden", b, i]
                if b == 0 and i == 0:
                    pe.wait_ge(ffn_w_lo, 8)
                pe.wait_ge(x2_hi, b + 1)
                for n, w in enumerate((w_gate, w_up)):
                    for k in range(2):
                        first = (2 * i + k) * P
                        ins = product(ps[:, 2 * n + k, :], [lambda c, h=h: w[h][:, c, first:first + P] for h in (0, 1)],
                                      [lambda c, h=h: x2t[h][:, c, :] for h in (0, 1)], range(EC),
                                      MOVING_LAST, x2_lo, b + 1)
                ins.then_inc(hidden_done, 1)

            def down(b, i):
                ps = place["down", b, i]
                if b == 0:
                    pe.wait_ge(ffn_w_lo, 12)
                for pair_ in range(FP):
                    chunks = (2 * pair_, 2 * pair_ + 1)
                    pe.wait_ge(g_hi, FP * b + pair_ + 1)
                    for t in range(TT):
                        for c in chunks:
                            for wn in range(2):
                                nc.tensor.matmul(ps[:, 2 * t, :], g[0][:, c, t * P:(t + 1) * P], w_down[wn][:, c, :],
                                                 start=(c == 0 and wn == 0), stop=False)
                    pe.wait_ge(g_lo, FP * b + pair_ + 1)
                    for t in range(TT):
                        for c in chunks:
                            ins = nc.tensor.matmul(ps[:, 2 * t, :], g[1][:, c, t * P:(t + 1) * P], w_down[0][:, c, :],
                                                   start=False, stop=(c == FC - 1))
                ins.then_inc(down_done, 1)

            pe.wait_ge(const_v, 1)
            for n in range(WARM_UP):
                nc.tensor.matmul(place["low", 0, 0][0:D, 0, :], ones[:, :], gat[:, 0, :], start=True, stop=True)

            do = {"low": low_proj, "value": value_proj, "squares": squares, "mixed": mixed, "scores": scores,
                  "turn_exp": turn_exp, "inverse": inverse, "context": context,
                  "turn_x": turn_x, "hidden": hidden, "down": down,
                  "decay": lambda b, i: high_proj("decay", b, i), "query": lambda b, i: high_proj("query", b, i)}
            for kind, b, i in in_order("pe"):
                wait_freed(pe, (kind, b, i))
                do[kind](b, i)

        @block.scalar
        def _(act):
            def high(hi, raw_, done):
                nc.scalar.activation(hi, raw_, ACT.Copy).then_inc(done, 1)

            def xt_high(b, i):
                s = b % 2
                act.wait_ge(in_xt[b], 16)
                if b >= 2:
                    act.wait_ge(value_done, 2 * (b - 1))
                    act.wait_ge(low_done, 2 * (b - 1))
                high(xt[0][:, s, :, :].rearrange("p c t -> p (c t)"), xt_raw[:, b, :], xt_hi)

            def w_high_high(b, i):
                act.wait_ge(in_high[i], 16)
                high(w_high[0][:, 1 - i, :], raw[1][:, (1 - i) * C:(2 - i) * C], high_w_hi)

            def w_v_high(b, i):
                act.wait_ge(in_v, 16)
                high(w_v[0][:, :, :].rearrange("p c n -> p (c n)"), raw[2], v_w_hi)

            def ffn_high(b, i):
                act.wait_ge(in_ffn[i], 16)
                high(ffn_chunk(i, 0, 4)[0], ffn_raw[i], ffn_w_hi)

            def x1_high(b, i):
                act.wait_ge(normed[0], b + 1)
                if b >= 1:
                    act.wait_ge(x_stacked, stacks * b)
                nc.scalar.activation(x1_h[0][:, :, :], res_i[:, b % 2, :, :], ACT.Copy).then_inc(x1_hi, 1)

            def low_high(b, i):
                ps = place["low", b, 0]
                w = 1 - i
                act.wait_ge(low_done, 2 * b + i + 1)
                if b >= 1:
                    act.wait_ge((decay_done, query_done)[i], 2 * b)
                nc.scalar.activation(low[0][:, w, :], ps[:, 2 * w, :], ACT.Copy).then_inc(low_hi, 1)

            def decay(b, i):
                ps = place["decay", b, 0]
                cs = slice(half(i)[0], half(i)[-1] + 1)
                act.wait_ge(decay_done, 2 * b + i + 1)
                if b >= 1:
                    act.wait_ge(state_done, CC * (b - 1) + CC // 2 * (i + 1))
                if b == 0:
                    act.wait_ge(const_v, 1)
                nc.scalar.activation(dec[:, cs, :], ps[:, cs, :], ACT.Tanh, scale=0.5).then_inc(tan1, 1)
                act.wait_ge(tan1, 2 * b + i + 1)
                nc.scalar.activation(dec[:, cs, :], dec[:, cs, :], ACT.Tanh, bias=quarter[:, 0:1], scale=0.25).then_inc(tan2, 1)
                act.wait_ge(tan2, 2 * b + i + 1)
                nc.scalar.activation(dec[:, cs, :], dec[:, cs, :], ACT.Copy, bias=0.5, scale=0.5).then_inc(a_done, 1)

            def query(b, i):
                ps = place["query", b, 0]
                cs = slice(half(i)[0], half(i)[-1] + 1)
                act.wait_ge(query_done, 2 * b + i + 1)
                if b >= 1:
                    act.wait_ge(out_done, 2 * b - 1 + i)
                nc.scalar.activation(gat[:, cs, :], ps[:, cs, :], ACT.Tanh, scale=0.5).then_inc(qtan, 1)

            def outputs(b, i):
                cs = slice(half(i)[0], half(i)[-1] + 1)
                act.wait_ge(out_done, 2 * b + i + 1)
                nc.scalar.activation(hid[:, cs, :], mix[:, cs, :], ACT.Square).then_inc(sq_done, 1)
                if b >= 1:
                    act.wait_ge(mixed_done, b)
                nc.scalar.activation(o[0][:, cs, :], mix[:, cs, :], ACT.Copy).then_inc(o_hi, 1)

            def exp(b, i):
                n = HP * b + i
                act.wait_ge(shift_done, n + 1)
                if n < 2:
                    act.wait_ge(ffn_w_lo, 2 * (n + 1))
                if n >= 2:
                    act.wait_ge(exp_turned, n - 1)
                if b >= 1:
                    act.wait_ge(inv_done, b)
                for h in range(2):
                    for c in range(EC):
                        ins = nc.scalar.activation(numer[:, n % 2, 2 * h + c, :], place["scores", b, i][:, 2 * h + c, :], ACT.Exp,
                                                   bias=shift[:, 2 * i + h, c:c + 1], scale=ATT_SCALE,
                                                   accum_out=total[:, 2 * i + h, c:c + 1])
                ins.then_inc(exp_done, 1)

            def keep_turned(b, i):
                act.wait_ge(exp_turned, HP * b + i + 1)
                if b == 0:
                    act.wait_ge(ffn_w_lo, 2 * (i + 3))
                if b >= 1:
                    act.wait_ge(context_done, b)
                nc.scalar.activation(prob[:, 2 * i, :, :], place["turn_exp", b, i][:, 0:2, :], ACT.Copy).then_inc(prob_even, 1)

            def keep_inverse(b, i):
                act.wait_ge(inv_turned, b + 1)
                if b >= 1:
                    act.wait_ge(added[1], b)
                nc.scalar.activation(inv_b[:, :, :], place["inverse", b, 0][:, :].rearrange("p (t e) -> p t e", t=TT),
                                     ACT.Copy).then_inc(inv_spread, 1)

            def x2_high(b, i):
                act.wait_ge(x_turned, b + 1)
                if b >= 1:
                    act.wait_ge(hidden_done, FP * b)
                nc.scalar.activation(x2t[0][:, :, :], place["turn_x", b, 0][:, :].rearrange("p (c t) -> p c t", c=EC),
                                     ACT.Copy).then_inc(x2_hi, 1)

            def gate(b, i):
                n = FP * b + i
                act.wait_ge(hidden_done, n + 1)
                if n >= 2:
                    act.wait_ge(g_lo, n - 1)
                    act.wait_ge(g_hi, n - 1)
                nc.scalar.activation(gu[:, n % 2, :].rearrange("p (k t) -> p k t", k=2),
                                     place["hidden", b, i][:, 0:2, :], ACT.Tanh, scale=0.5).then_inc(gtan, 1)

            def g_high(b, i):
                n = FP * b + i
                act.wait_ge(g_done, n + 1)
                if b >= 1:
                    act.wait_ge(down_done, b)
                nc.scalar.activation(g[0][:, 2 * i:2 * i + 2, :], gu[:, n % 2, :].rearrange("p (k t) -> p k t", k=2),
                                     ACT.Copy).then_inc(g_hi, 1)

            do = {"w_high": w_high_high, "w_v": w_v_high, "xt": xt_high, "x1": x1_high, "low": low_high, "decay": decay, "query": query, "outputs": outputs, "weights": ffn_high,
                  "exp": exp, "turned": keep_turned, "inverse": keep_inverse, "x2": x2_high, "gate": gate, "g": g_high}
            for kind, b, i in in_order("act"):
                do[kind](b, i)

        @block.vector
        def _(dve):
            nc.vector.memset(quarter[:, :], 0.25)
            nc.vector.memset(gat[:, 0, :], 0.0)
            nc.vector.memset(ones[:, :], 1.0).then_inc(const_v, 1)

            def rest(halves_, pattern, raw_, done):
                hi, lo = (x.rearrange(pattern) for x in halves_)
                nc.vector.tensor_tensor(lo, raw_, hi, ALU.subtract).then_inc(done, 1)

            def split_xt(b, i):
                s = b % 2
                dve.wait_ge(xt_hi, b + 1)
                rest([x[:, s, :, :] for x in xt], "p c t -> p (c t)", xt_raw[:, b, :], xt_lo)

            def w_low_both(b, i):
                dve.wait_ge(in_low, 16)
                nc.vector.tensor_copy(w_low[0][:, :, :, :].rearrange("p w c n -> p (w c n)"), low_raw).then_inc(low_w_hi, 1)
                dve.wait_ge(low_w_hi, 1)
                rest([x[:, :, :, :] for x in w_low], "p w c n -> p (w c n)", low_raw, low_w_lo)

            def w_high_rest(b, i):
                dve.wait_ge(high_w_hi, i + 1)
                nc.vector.tensor_tensor(w_high[1][:, 1 - i, :], raw[1][:, (1 - i) * C:(2 - i) * C], w_high[0][:, 1 - i, :],
                                        ALU.subtract).then_inc(high_w_lo, 1)

            def w_v_rest(b, i):
                dve.wait_ge(v_w_hi, 1)
                rest([x[:, :, :] for x in w_v], "p c n -> p (c n)", raw[2], v_w_lo)

            def low_rest(b, i):
                ps = place["low", b, 0]
                w = 1 - i
                dve.wait_ge(low_hi, 2 * b + i + 1)
                nc.vector.tensor_tensor(low[1][:, w, :], ps[:, 2 * w, :], low[0][:, w, :],
                                        ALU.subtract).then_inc(low_lo, 1)

            def recur(b, i):
                cs = slice(half(i)[0], half(i)[-1] + 1)
                n = 2 * b + i
                dve.wait_ge(a_done, n + 1)
                if b >= 1:
                    dve.wait_ge(squares_done, b)
                dve.wait_ge(value_done, n + 1)
                nc.vector.scalar_tensor_tensor(out=hid[:, cs, :], in0=dec[:, cs, :], scalar=1.0, in1=place["value", b, 0][:, cs, :],
                                               op0=ALU.subtract, op1=ALU.mult).then_inc(kv_done, 1)
                dve.wait_ge(kv_done, n + 1)
                for cc in half(i):
                    nc.vector.tensor_tensor_scan(hid[:, cc, :], dec[:, cc, :], hid[:, cc, :], 0.0, ALU.mult,
                                                 ALU.subtract).then_inc(state_done, 1)

            def silu(b, i):
                cs = slice(half(i)[0], half(i)[-1] + 1)
                n = 2 * b + i
                dve.wait_ge(qtan, n + 1)
                nc.vector.scalar_tensor_tensor(out=gat[:, cs, :], in0=gat[:, cs, :], scalar=1.0, in1=place["query", b, 0][:, cs, :],
                                               op0=ALU.add, op1=ALU.mult).then_inc(silu_done, 1)
                dve.wait_ge(silu_done, n + 1)
                dve.wait_ge(state_done, CC * b + CC // 2 * (i + 1))
                if b >= 1:
                    dve.wait_ge(sq_done, n - 1)
                    dve.wait_ge(o_hi, n - 1)
                    dve.wait_ge(o_lo, n - 1)
                for cc in half(i):
                    ins = nc.vector.tensor_tensor(mix[:, cc, :].rearrange("p (t d j) -> p t j d", t=TT, j=Q),
                                                  gat[:, cc, :].rearrange("p (t j d) -> p t j d", t=TT, j=Q),
                                                  hid[:, cc, :].rearrange("p (t j d) -> p t j d", t=TT, j=Q), ALU.mult)
                ins.then_inc(out_done, 1)

            def turn_squares(b, i):
                dve.wait_ge(squares_done, b + 1)
                if b >= 1:
                    dve.wait_ge(ms_done, b)
                nc.vector.transpose(sq_t[:, :, :].rearrange("p t d -> p (t d)"), place["squares", b, 0][:, 0:TT * 32]).then_inc(sq_turned, 1)

            def norm_stats(n, b, tile):
                if b >= 1:
                    dve.wait_ge(mv_done[n], TT * b)
                for t in range(TT):
                    nc.vector.bn_stats(bn[:, n, t, :], tile[:, t, :]).then_inc(bn_done[n], 1)
                if b >= 1:
                    dve.wait_ge(normed[n], b)
                for t in range(TT):
                    dve.wait_ge(bn_done[n], TT * b + t + 1)
                    nc.vector.bn_aggr(mv[:, n, t, :], bn[:, n, t, :]).then_inc(mv_done[n], 1)

            def norm_apply(n, b, tile):
                dve.wait_ge(rstd_done[n], b + 1)
                for t in range(TT):
                    ins = nc.vector.tensor_scalar(tile[:, t, :], tile[:, t, :], mv[:, n, t, 0:1], rstd[:, n, t:t + 1],
                                                  ALU.subtract, ALU.mult)
                ins.then_inc(normed[n], 1)

            def add_mixed(b, i):
                dve.wait_ge(mixed_done, b + 1)
                dve.wait_ge(rms_done, b + 1)
                dve.wait_ge(in_x[b % 2], 16 * (b // 2 + 1))
                x_i = res_i[:, b % 2, :, :]
                for t in range(TT):
                    ins = nc.vector.scalar_tensor_tensor(out=x_i[:, t, :], in0=place["mixed", b, 0][:, t * E:(t + 1) * E],
                                                         scalar=rms[:, t:t + 1], in1=x_i[:, t, :],
                                                         op0=ALU.mult, op1=ALU.add)
                ins.then_inc(added[0], 1)
                dve.wait_ge(added[0], b + 1)
                norm_stats(0, b, x_i)

            def norm1(b, i):
                x_i = res_i[:, b % 2, :, :]
                norm_apply(0, b, x_i)

            def x1_rest(b, i):
                dve.wait_ge(x1_hi, b + 1)
                nc.vector.tensor_tensor(x1_h[1][:, :, :], res_i[:, b % 2, :, :], x1_h[0][:, :, :], ALU.subtract).then_inc(x1_lo, 1)

            def maximum(b, i):
                dve.wait_ge(scores_done, HP * b + i + 1)
                if b >= 1:
                    dve.wait_ge(shift_done, HP * (b - 1) + i + 1)
                nc.vector.tensor_reduce(top[:, 2 * i:2 * i + 2, :].rearrange("p h c -> p (h c)"), place["scores", b, i][:, :, :],
                                        AX_X, ALU.max).then_inc(top_done, 1)

            def keep_turned(b, i):
                dve.wait_ge(exp_turned, HP * b + i + 1)
                if b == 0:
                    dve.wait_ge(ffn_w_lo, 2 * (i + 3))
                if b >= 1:
                    dve.wait_ge(context_done, b)
                nc.vector.tensor_copy(prob[:, 2 * i + 1, :, :], place["turn_exp", b, i][:, 2:4, :]).then_inc(prob_odd, 1)

            def invert(b, i):
                dve.wait_ge(exp_done, HP * (b + 1))
                if b >= 1:
                    dve.wait_ge(inv_widened, b)
                nc.vector.reciprocal(inv[:, :, :], total[:, :, :]).then_inc(inv_done, 1)

            def weigh(b, i):
                dve.wait_ge(context_done, b + 1)
                dve.wait_ge(inv_spread, b + 1)
                nc.vector.tensor_tensor(inv_b[:, :, :], place["context", b, 0][:, :].rearrange("p (t e) -> p t e", t=TT),
                                        inv_b[:, :, :], ALU.mult).then_inc(weighed, 1)
                dve.wait_ge(weighed, b + 1)
                dve.wait_ge(x_moved[b], 16)
                nc.vector.tensor_tensor(res[:, b, :, :], res[:, b, :, :], inv_b[:, :, :], ALU.add).then_inc(added[1], 1)
                dve.wait_ge(added[1], b + 1)
                norm_stats(1, b, res[:, b, :, :])

            def norm2(b, i):
                norm_apply(1, b, res[:, b, :, :])

            def x2_rest(b, i):
                dve.wait_ge(x2_hi, b + 1)
                nc.vector.tensor_tensor(x2t[1][:, :, :], place["turn_x", b, 0][:, :].rearrange("p (c t) -> p c t", c=EC),
                                        x2t[0][:, :, :], ALU.subtract).then_inc(x2_lo, 1)

            def gate(b, i):
                n = FP * b + i
                ps = place["hidden", b, i]
                v = gu[:, n % 2, :].rearrange("p (k t) -> p k t", k=2)
                dve.wait_ge(gtan, n + 1)
                nc.vector.scalar_tensor_tensor(out=v, in0=v, scalar=1.0, in1=ps[:, 0:2, :], op0=ALU.add,
                                               op1=ALU.mult).then_inc(gate_done, 1)
                dve.wait_ge(gate_done, n + 1)
                nc.vector.tensor_tensor(v, v, ps[:, 2:4, :], ALU.mult).then_inc(g_done, 1)

            def g_rest(b, i):
                n = FP * b + i
                dve.wait_ge(g_hi, n + 1)
                dve.wait_ge(g_lo, n)
                if b >= 1:
                    dve.wait_ge(down_done, b)
                nc.vector.tensor_tensor(g[1][:, 2 * i:2 * i + 2, :], gu[:, n % 2, :].rearrange("p (k t) -> p k t", k=2),
                                        g[0][:, 2 * i:2 * i + 2, :], ALU.subtract).then_inc(g_lo, 1)

            def add_down(b, i):
                dve.wait_ge(down_done, b + 1)
                dve.wait_ge(normed[1], b + 1)
                nc.vector.scalar_tensor_tensor(out=res[:, b, :, :], in0=place["down", b, 0][:, 0:2 * TT:2, :], scalar=0.5,
                                               in1=res[:, b, :, :], op0=ALU.mult, op1=ALU.add).then_inc(added[2], 1)
                dve.wait_ge(added[2], b + 1)
                norm_stats(2, b, res[:, b, :, :])

            def norm3(b, i):
                norm_apply(2, b, res[:, b, :, :])

            do = {"w_low": w_low_both, "w_high": w_high_rest, "w_v": w_v_rest, "xt": split_xt, "low": low_rest, "recur": recur, "silu": silu, "squares": turn_squares,
                  "mixed": add_mixed, "x1": x1_rest, "norm1": norm1, "max": maximum, "turned": keep_turned, "invert": invert,
                  "weigh": weigh, "norm2": norm2, "x2": x2_rest, "gate": gate, "g": g_rest, "down": add_down, "norm3": norm3}
            for kind, b, i in in_order("dve"):
                do[kind](b, i)

        @block.gpsimd
        def _(pool):
            nc.gpsimd.memset(ident[:, :], 0.0).then_inc(consts, 1)
            nc.gpsimd.memset(power[:, :], -0.5).then_inc(consts, 1)
            pool.wait_ge(consts, 2)
            nc.gpsimd.affine_select(out=ident[:, :], in_=ident[:, :], compare_op=ALU.not_equal, fill=1.0, base=0,
                                    pattern=[[-1, P]], channel_multiplier=1).then_inc(consts, 1)
            pool.wait_ge(consts, 3)

            def same(out, in_):
                return nc.gpsimd.tensor_scalar(out, in_, 1.0, 0.0, ALU.mult, ALU.add)

            def split_ctx(b):
                pool.wait_ge(in_ctx, 16 * (b + 1))
                if b >= 1:
                    pool.wait_ge(ctx_stacked, stacks * b)
                same(ctx_h[0][:, :, :], ctx_raw[:, :, :]).then_inc(ctx_hi, 1)
                pool.wait_ge(ctx_hi, b + 1)
                nc.gpsimd.tensor_tensor(ctx_h[1][:, :, :], ctx_raw[:, :, :], ctx_h[0][:, :, :], ALU.subtract).then_inc(ctx_lo, 1)

            def split_wo():
                pool.wait_ge(in_norm, 16)
                pool.wait_ge(in_o, 16)
                ro = raw[3].rearrange("p (c n) -> p c n", c=CC)
                for c in range(CC):
                    nc.gpsimd.tensor_scalar(ro[:, c, :], ro[:, c, :], normw[:, c:c + 1], 1.0, ALU.mult, ALU.mult).then_inc(o_scaled, 1)
                pool.wait_ge(o_scaled, CC)
                same(w_o[0][:, :, :], ro).then_inc(o_w_hi, 1)
                pool.wait_ge(o_w_hi, 1)
                nc.gpsimd.tensor_tensor(w_o[1][:, :, :], ro, w_o[0][:, :, :], ALU.subtract).then_inc(o_w_lo, 1)

            def ffn_rest(b, i):
                pool.wait_ge(ffn_w_hi, i // 2 + 1)
                first = 2 * (i % 2)
                hi, lo = ffn_chunk(i // 2, first, first + 2)
                nc.gpsimd.tensor_tensor(lo, ffn_raw[i // 2][:, first * E:(first + 2) * E], hi, ALU.subtract).then_inc(ffn_w_lo, 1)

            def outputs(b, i):
                cs = slice(half(i)[0], half(i)[-1] + 1)
                pool.wait_ge(o_hi, 2 * b + i + 1)
                if b >= 1:
                    pool.wait_ge(mixed_done, b)
                nc.gpsimd.tensor_tensor(o[1][:, cs, :], mix[:, cs, :], o[0][:, cs, :], ALU.subtract).then_inc(o_lo, 1)

            def shift_of(b, i):
                pool.wait_ge(top_done, HP * b + i + 1)
                if b >= 1:
                    pool.wait_ge(exp_done, HP * (b - 1) + i + 1)
                nc.gpsimd.tensor_scalar(shift[:, 2 * i:2 * i + 2, :].rearrange("p h c -> p (h c)"),
                                        top[:, 2 * i:2 * i + 2, :].rearrange("p h c -> p (h c)"), -ATT_SCALE, 0.0,
                                        ALU.mult, ALU.add).then_inc(shift_done, 1)

            def xt_rest(b, i):
                pool.wait_ge(xt_hi, b + 1)
                pool.wait_ge(xt_lo, b)
                if b >= 2:
                    pool.wait_ge(value_done, 2 * (b - 1))
                    pool.wait_ge(low_done, 2 * (b - 1))
                nc.gpsimd.tensor_tensor(xt[1][:, b % 2, :, :].rearrange("p c t -> p (c t)"), xt_raw[:, b, :],
                                        xt[0][:, b % 2, :, :].rearrange("p c t -> p (c t)"), ALU.subtract).then_inc(xt_lo, 1)

            def widen(b, i):
                pool.wait_ge(inv_done, b + 1)
                if b >= 1:
                    pool.wait_ge(inv_turned, b)
                nc.gpsimd.tensor_scalar(inv_wide[:, :, :, :, :],
                                        inv[:, :, :].rearrange("p (j t) c -> p t c j", t=TT).unsqueeze(4)
                                        .to_broadcast([P, TT, EC, Q, D]), 1.0, 0.0, ALU.mult, ALU.add).then_inc(inv_widened, 1)

            def inv_root(out, var, factor, eps, ve_, done_ve, done, b):
                nc.gpsimd.tensor_scalar(ve_, var, factor, eps, ALU.mult, ALU.add).then_inc(done_ve, 1)
                pool.wait_ge(done_ve, b + 1)
                nc.gpsimd.tensor_tensor(out, ve_, power[:, :], ALU.pow).then_inc(done, 1)

            def rms_root(b, i):
                pool.wait_ge(sq_turned, b + 1)
                if b >= 1:
                    pool.wait_ge(added[0], b)
                inv_root(rms[:, :], sq_t[:, :, 0], 1.0 / C, 4 * RMS_EPS, ms[:, :], ms_done, rms_done, b)

            def norm_root(n, b):
                pool.wait_ge(mv_done[n], TT * (b + 1))
                if b >= 1:
                    pool.wait_ge(normed[n], b)
                inv_root(rstd[:, n, :], mv[:, n, :, 1], 1.0, LN_EPS, ve[:, n, :], ve_done[n], rstd_done[n], b)

            def g_rest(b, i):
                n = FP * b + i
                pool.wait_ge(g_hi, n + 1)
                nc.gpsimd.tensor_tensor(g[1][:, 2 * i:2 * i + 2, :], gu[:, n % 2, :].rearrange("p (k t) -> p k t", k=2),
                                        g[0][:, 2 * i:2 * i + 2, :], ALU.subtract).then_inc(g_lo, 1)

            do = {"outputs": outputs, "rms": rms_root, "norm1": lambda b, i: norm_root(0, b),
                  "norm2": lambda b, i: norm_root(1, b), "norm3": lambda b, i: norm_root(2, b), "g": g_rest,
                  "weights": ffn_rest, "wo": lambda b, i: split_wo(), "widen": widen, "shift": shift_of, "xt": xt_rest,
                  "ctx": lambda b, i: split_ctx(b)}
            for kind, b, i in in_order("pool"):
                do[kind](b, i)


def kernel(x, ctx_2048, L0_attn_Wq1, L0_attn_Wq2, L0_attn_Wk1, L0_attn_Wk2, L0_attn_Wv, L0_attn_Wo,
           L0_attn_norm_w, L0_ffn_w_gate, L0_ffn_w_up, L0_ffn_w_down):
    import concourse.bacc as bacc
    import numpy as np
    from concourse.bass_utils import run_bass_kernel_spmd

    def rows(w):
        return w.reshape(-1, P, w.shape[-1]).transpose(1, 0, 2).reshape(P, -1)

    def channels(z):
        return z.transpose(0, 2, 1).reshape(B, EC, P, T).transpose(0, 2, 1, 3).reshape(B, P, EC * T)

    def interleaved(z):
        return z.reshape(B, TT, Q, D, E).transpose(0, 3, 2, 1, 4).reshape(B, P, TT * E)

    x, c = np.asarray(x), np.asarray(ctx_2048)
    wq1, wk1, wq2, wk2, wv, wo, norm_w, gate, up, down = (np.asarray(w) for w in (
        L0_attn_Wq1, L0_attn_Wk1, L0_attn_Wq2, L0_attn_Wk2, L0_attn_Wv, L0_attn_Wo, L0_attn_norm_w,
        L0_ffn_w_gate, L0_ffn_w_up, L0_ffn_w_down))
    arrays = {
        "xT": channels(x),
        "x": interleaved(x),
        "ctx": interleaved(c),
        "ctxT": channels(c),
        "w1": np.concatenate([rows(wq1), rows(wk1)], axis=1),
        "w2": np.concatenate([wq2, wk2], axis=1),
        "wv": rows(wv),
        "wo": rows(wo),
        "norm": norm_w.reshape(CC, P).T,
        "w_ffn": np.concatenate([rows(gate.T), rows(up.T), rows(down.T)], axis=1).reshape(P, 6, 1024),
    }
    arrays = {k: np.ascontiguousarray(v) for k, v in arrays.items()}
    nc = bacc.Bacc("TRN2", target_bir_lowering=False, num_devices=1)
    args = [nc.dram_tensor(k, v.shape, F32, kind="ExternalInput").ap() for k, v in arrays.items()]
    out = nc.dram_tensor("out", (B, T, E), F32, kind="ExternalOutput").ap()
    x1_dram = nc.dram_tensor("x1_dram", (B, P, TT * E), F32, kind="Internal").ap()
    decoder_layer(nc, *args, out, x1_dram)
    r = run_bass_kernel_spmd(nc, [arrays], core_ids=[0])
    return r.results[0]["out"]
```
